# Optimizing a Trainium2 kernel written in Bass

```python
import numpy as np
import jax
import jax.numpy as jnp

def _softmax(x, axis=-1):
    return jax.nn.softmax(x, axis=axis)

def _gelu(x):
    return jax.nn.gelu(x, approximate=True)

def _silu(x):
    return jax.nn.silu(x)

def _sigmoid(x):
    return jax.nn.sigmoid(x)

def _layernorm(x, axis=-1, eps=1e-05):
    m = jnp.mean(x, axis=axis, keepdims=True)
    v = jnp.var(x, axis=axis, keepdims=True)
    return (x - m) / jnp.sqrt(v + eps)

def _scatter_add(tgt, idx, src, axis=0):
    return tgt.at[idx].add(src)

def _segment_sum(src, seg, n):
    return jax.ops.segment_sum(src, seg, n)
kernel_name = 'mk_decoder_preln_d2_seqx_r4_9d490a'

def setup_inputs(seed: int=0):
    np.random.seed(seed)
    _w = jnp.asarray

    def _rec_inputs():
        import jax
        import jax.numpy as jnp
        _rk = jax.random.key(seed)
        x = -0.0003929 + 0.9999 * jax.random.normal(jax.random.fold_in(_rk, 1), (2, 1024, 256), jnp.float32)
        _lenS = 1024 - jax.random.randint(jax.random.fold_in(_rk, 7), (2,), 0, max(1, 1024 // 4) + 1, jnp.int32)
        _lenS2 = 77 - jax.random.randint(jax.random.fold_in(_rk, 8), (2,), 0, max(1, 77 // 4) + 1, jnp.int32)
        _ctx_1024P = jax.random.normal(jax.random.fold_in(_rk, 11), (2, 16, 256), jnp.float32)
        _ctx_1024c = jax.random.dirichlet(jax.random.fold_in(_rk, 511), 0.3 * jnp.ones((16,), jnp.float32), (2, 77))
        _ctx_1024t = jnp.einsum('bsk,bkd->bsd', _ctx_1024c, _ctx_1024P)
        _ctx_1024t = _ctx_1024t * jax.lax.rsqrt(jnp.mean(jnp.square(_ctx_1024t)) + 1e-12) * 0.953939
        ctx_1024 = 2.81802e-05 + 1.00001 * (_ctx_1024t + 0.3 * jax.random.normal(jax.random.fold_in(_rk, 611), (2, 77, 256), jnp.float32))
        _validS = jnp.arange(1024)[None, :] < _lenS[:, None]
        _validS2 = jnp.arange(77)[None, :] < _lenS2[:, None]
        _causal = jnp.tril(jnp.ones((1024, 1024), dtype=bool))
        mask_BxS2_ff1 = jnp.where(jnp.ones((2, 77), dtype=bool), 1.0, 0.0).astype(jnp.float32)
        return (x, ctx_1024, mask_BxS2_ff1)
    x, ctx_1024, mask_BxS2_ff1 = _rec_inputs()

    def _L0_attn_setup():
        import jax, jax.numpy as jnp
        import numpy as np
        HIDDEN = 256
        HEADS = 16
        HEAD_DIM = HIDDEN // HEADS
        MAX_SEQ = 512

        def _rope_tables():
            inv_freq = 1.0 / 10000.0 ** (jnp.arange(0, HEAD_DIM, 2, dtype=jnp.float32) / HEAD_DIM)
            t = jnp.arange(MAX_SEQ, dtype=jnp.float32)
            freqs = t[:, None] * inv_freq[None, :]
            return (jnp.cos(freqs), jnp.sin(freqs))
        key = jax.random.key(seed)
        k1, k2, k3 = jax.random.split(key, 3)
        x = jax.random.normal(k1, (2, 512, HIDDEN), dtype=jnp.float32)
        qkv_w = jax.random.normal(k2, (HIDDEN, 3 * HIDDEN), dtype=jnp.float32) * 0.02
        qkv_b = jnp.zeros((3 * HIDDEN,), dtype=jnp.float32)
        out_w = jax.random.normal(k3, (HIDDEN, HIDDEN), dtype=jnp.float32) * 0.02
        out_b = jnp.zeros((HIDDEN,), dtype=jnp.float32)
        return {'x': x, 'qkv_w': qkv_w, 'qkv_b': qkv_b, 'out_w': out_w, 'out_b': out_b}
    _L0_attn_all = _L0_attn_setup()
    _L0_attn_in = {k: v for k, v in _L0_attn_all.items() if k in ('qkv_w', 'qkv_b', 'out_w', 'out_b')}
    del _L0_attn_all

    def _L0_xattn_setup():
        import jax, jax.numpy as jnp
        import numpy as np
        D_MODEL = 256
        HEADS = 16
        DEPTH = D_MODEL // HEADS
        B, S = (4, 1024)
        EPS_K = 1e-06
        EPS_LN = 1e-06

        def _layernorm(x, g, b):
            m = jnp.mean(x, axis=-1, keepdims=True)
            var = jnp.var(x, axis=-1, keepdims=True)
            return (x - m) * jax.lax.rsqrt(var + EPS_LN) * g + b

        def _split_heads(x):
            bsz, sl, _ = x.shape
            return x.reshape(bsz, sl, HEADS, DEPTH).transpose(0, 2, 1, 3)
        key = jax.random.key(seed)
        ks = jax.random.split(key, 8)
        lecun = 1.0 / np.sqrt(D_MODEL)
        glorot = np.sqrt(2.0 / (D_MODEL + D_MODEL))
        return {'q': jax.random.normal(ks[0], (B, S, D_MODEL), jnp.float32), 'k': jax.random.normal(ks[1], (B, S, D_MODEL), jnp.float32), 'v': jax.random.normal(ks[2], (B, S, D_MODEL), jnp.float32), 'mask': jnp.ones((B, S), jnp.float32), 'wq': jax.random.normal(ks[3], (D_MODEL, D_MODEL), jnp.float32) * lecun, 'wk': jax.random.normal(ks[4], (D_MODEL, D_MODEL), jnp.float32) * lecun, 'wv': jax.random.normal(ks[5], (D_MODEL, D_MODEL), jnp.float32) * lecun, 'ln_gamma': jnp.ones((D_MODEL,), jnp.float32), 'ln_beta': jnp.zeros((D_MODEL,), jnp.float32), 'dense_w': jax.random.normal(ks[6], (D_MODEL, D_MODEL), jnp.float32) * glorot, 'dense_b': jnp.zeros((D_MODEL,), jnp.float32)}
    _L0_xattn_all = _L0_xattn_setup()
    _L0_xattn_in = {k: v for k, v in _L0_xattn_all.items() if k in ('wq', 'wk', 'wv', 'ln_gamma', 'ln_beta', 'dense_w', 'dense_b')}
    del _L0_xattn_all

    def _L0_ffn_setup():
        import jax, jax.numpy as jnp
        import numpy as np
        BLOCK = 32
        W_BITS = 4
        ACT_BITS = 16

        def act_qdq(x):
            qmax = 2.0 ** (ACT_BITS - 1) - 1.0
            scale = jnp.maximum(jnp.max(jnp.abs(x)) / qmax, 1e-12)
            return jnp.clip(jnp.round(x / scale), -qmax - 1.0, qmax) * scale

        def fixed_qdq_u16(x):
            scale = 1.0 / 65536.0
            return jnp.clip(jnp.round(x / scale), 0.0, 65535.0) * scale

        def lpbq_dequant(w):
            O, I = w.shape
            qmax = 2.0 ** (W_BITS - 1) - 1.0
            wb = w.reshape(O, I // BLOCK, BLOCK)
            s = jnp.maximum(jnp.max(jnp.abs(wb), axis=-1, keepdims=True) / qmax, 1e-12)
            wq = jnp.clip(jnp.round(wb / s), -qmax - 1.0, qmax) * s
            return wq.reshape(O, I)
        key = jax.random.key(seed)
        k1, k2, k3, k4 = jax.random.split(key, 4)
        B, S, H, I = (2, 1024, 256, 768)
        x = jax.random.normal(k1, (B, S, H), jnp.float32)
        w_gate = jax.random.normal(k2, (I, H), jnp.float32) * 0.02
        w_up = jax.random.normal(k3, (I, H), jnp.float32) * 0.02
        w_down = jax.random.normal(k4, (H, I), jnp.float32) * 0.02
        return {'x': x, 'w_gate': w_gate, 'w_up': w_up, 'w_down': w_down}
    _L0_ffn_all = _L0_ffn_setup()
    _L0_ffn_in = {k: v for k, v in _L0_ffn_all.items() if k in ('w_gate', 'w_up', 'w_down')}
    del _L0_ffn_all

    def _L1_attn_setup():
        import jax, jax.numpy as jnp
        import numpy as np
        H = 16
        key = jax.random.key(seed)
        k1, k2, k3 = jax.random.split(key, 3)
        B, S, E = (2, 512, 256)
        return {'hidden_states': jax.random.normal(k1, (B, S, E), dtype=jnp.float32), 'W_attn': jax.random.normal(k2, (E, 3 * E), dtype=jnp.float32) * 0.02, 'b_attn': jnp.zeros((3 * E,), dtype=jnp.float32), 'W_proj': jax.random.normal(k3, (E, E), dtype=jnp.float32) * 0.02, 'b_proj': jnp.zeros((E,), dtype=jnp.float32)}
    _L1_attn_all = _L1_attn_setup()
    _L1_attn_in = {k: v for k, v in _L1_attn_all.items() if k in ('W_attn', 'b_attn', 'W_proj', 'b_proj')}
    del _L1_attn_all

    def _L1_xattn_setup():
        import jax, jax.numpy as jnp
        import numpy as np
        EMBED_DIM = 256
        B, QL, KL = (4, 512, 512)
        key = jax.random.key(seed)
        k1, k2, k3, k4 = jax.random.split(key, 4)
        hidden_states = jax.random.normal(k1, (B, QL, EMBED_DIM), dtype=jnp.float32)
        decoder_hidden_states = jax.random.normal(k2, (B, KL, EMBED_DIM), dtype=jnp.float32)
        Wq = jax.random.normal(k3, (EMBED_DIM, EMBED_DIM), dtype=jnp.float32) * (1.0 / np.sqrt(EMBED_DIM))
        Wkv = jax.random.normal(k4, (EMBED_DIM, 2 * EMBED_DIM), dtype=jnp.float32) * (1.0 / np.sqrt(EMBED_DIM))
        return {'hidden_states': hidden_states, 'decoder_hidden_states': decoder_hidden_states, 'Wq': Wq, 'Wkv': Wkv}
    _L1_xattn_all = _L1_xattn_setup()
    _L1_xattn_in = {k: v for k, v in _L1_xattn_all.items() if k in ('Wq', 'Wkv')}
    del _L1_xattn_all

    def _L1_ffn_setup():
        import jax, jax.numpy as jnp
        import numpy as np
        EMBED_DIM = 256
        NUM_EXPERTS = 8
        B, S = (2, 512)
        key = jax.random.key(seed)
        ks = jax.random.split(key, 5)
        scale = 1.0 / np.sqrt(EMBED_DIM)
        x = jax.random.normal(ks[0], (B, S, EMBED_DIM), dtype=jnp.float32)
        router_w = jax.random.normal(ks[1], (NUM_EXPERTS, EMBED_DIM), dtype=jnp.float32) * scale
        router_b = jnp.zeros((NUM_EXPERTS,), dtype=jnp.float32)
        expert_w = jax.random.normal(ks[2], (NUM_EXPERTS, EMBED_DIM, EMBED_DIM), dtype=jnp.float32) * scale
        expert_b = jnp.zeros((NUM_EXPERTS, EMBED_DIM), dtype=jnp.float32)
        return {'x': x, 'router_w': router_w, 'router_b': router_b, 'expert_w': expert_w, 'expert_b': expert_b}
    _L1_ffn_all = _L1_ffn_setup()
    _L1_ffn_in = {k: v for k, v in _L1_ffn_all.items() if k in ('router_w', 'router_b', 'expert_w', 'expert_b')}
    del _L1_ffn_all
    return {'x': x, 'ctx_1024': ctx_1024, 'mask_BxS2_ff1': mask_BxS2_ff1, 'L0_attn_qkv_w': _L0_attn_in['qkv_w'], 'L0_attn_qkv_b': _L0_attn_in['qkv_b'], 'L0_attn_out_w': _L0_attn_in['out_w'], 'L0_attn_out_b': _L0_attn_in['out_b'], 'L0_xattn_wq': _L0_xattn_in['wq'], 'L0_xattn_wk': _L0_xattn_in['wk'], 'L0_xattn_wv': _L0_xattn_in['wv'], 'L0_xattn_ln_gamma': _L0_xattn_in['ln_gamma'], 'L0_xattn_ln_beta': _L0_xattn_in['ln_beta'], 'L0_xattn_dense_w': _L0_xattn_in['dense_w'], 'L0_xattn_dense_b': _L0_xattn_in['dense_b'], 'L0_ffn_w_gate': _L0_ffn_in['w_gate'], 'L0_ffn_w_up': _L0_ffn_in['w_up'], 'L0_ffn_w_down': _L0_ffn_in['w_down'], 'L1_attn_W_attn': _L1_attn_in['W_attn'], 'L1_attn_b_attn': _L1_attn_in['b_attn'], 'L1_attn_W_proj': _L1_attn_in['W_proj'], 'L1_attn_b_proj': _L1_attn_in['b_proj'], 'L1_xattn_Wq': _L1_xattn_in['Wq'], 'L1_xattn_Wkv': _L1_xattn_in['Wkv'], 'L1_ffn_router_w': _L1_ffn_in['router_w'], 'L1_ffn_router_b': _L1_ffn_in['router_b'], 'L1_ffn_expert_w': _L1_ffn_in['expert_w'], 'L1_ffn_expert_b': _L1_ffn_in['expert_b']}

def reference(x, ctx_1024, mask_BxS2_ff1, L0_attn_qkv_w, L0_attn_qkv_b, L0_attn_out_w, L0_attn_out_b, L0_xattn_wq, L0_xattn_wk, L0_xattn_wv, L0_xattn_ln_gamma, L0_xattn_ln_beta, L0_xattn_dense_w, L0_xattn_dense_b, L0_ffn_w_gate, L0_ffn_w_up, L0_ffn_w_down, L1_attn_W_attn, L1_attn_b_attn, L1_attn_W_proj, L1_attn_b_proj, L1_xattn_Wq, L1_xattn_Wkv, L1_ffn_router_w, L1_ffn_router_b, L1_ffn_expert_w, L1_ffn_expert_b):
    import jax
    import jax.numpy as jnp

    def _L0_attn_ref(x, qkv_w, qkv_b, out_w, out_b):
        import jax, jax.numpy as jnp
        import numpy as np
        HIDDEN = 256
        HEADS = 16
        HEAD_DIM = HIDDEN // HEADS
        MAX_SEQ = 512

        def _rope_tables():
            inv_freq = 1.0 / 10000.0 ** (jnp.arange(0, HEAD_DIM, 2, dtype=jnp.float32) / HEAD_DIM)
            t = jnp.arange(MAX_SEQ, dtype=jnp.float32)
            freqs = t[:, None] * inv_freq[None, :]
            return (jnp.cos(freqs), jnp.sin(freqs))
        b, s, _ = x.shape
        qkv = x @ qkv_w + qkv_b
        qkv = qkv.reshape(b, s, HEADS, 3 * HEAD_DIM).transpose(0, 2, 1, 3)
        q, k, v = jnp.split(qkv, 3, axis=-1)
        cos_tab, sin_tab = _rope_tables()
        cos = cos_tab[:HEADS][None, :, None, :]
        sin = sin_tab[:HEADS][None, :, None, :]

        def rot(u):
            u1 = u[..., :HEAD_DIM // 2]
            u2 = u[..., HEAD_DIM // 2:]
            return jnp.concatenate([u1 * cos - u2 * sin, u2 * cos + u1 * sin], axis=-1)
        q = rot(q)
        k = rot(k)
        scores = jnp.einsum('bhqd,bhkd->bhqk', q, k) / HEAD_DIM ** 0.5
        attn = jax.nn.softmax(scores.astype(jnp.float32), axis=-1).astype(scores.dtype)
        out = jnp.einsum('bhqk,bhkd->bhqd', attn, v)
        out = out.transpose(0, 2, 1, 3).reshape(b, s, HEADS * HEAD_DIM)
        return out @ out_w + out_b

    def _L0_xattn_ref(q, k, v, mask, wq, wk, wv, ln_gamma, ln_beta, dense_w, dense_b):
        import jax, jax.numpy as jnp
        import numpy as np
        D_MODEL = 256
        HEADS = 16
        DEPTH = D_MODEL // HEADS
        B, S = (4, 1024)
        EPS_K = 1e-06
        EPS_LN = 1e-06

        def _layernorm(x, g, b):
            m = jnp.mean(x, axis=-1, keepdims=True)
            var = jnp.var(x, axis=-1, keepdims=True)
            return (x - m) * jax.lax.rsqrt(var + EPS_LN) * g + b

        def _split_heads(x):
            bsz, sl, _ = x.shape
            return x.reshape(bsz, sl, HEADS, DEPTH).transpose(0, 2, 1, 3)
        bsz = q.shape[0]
        em = mask[:, None, :, None]
        qh = _split_heads(_layernorm(q @ wq, ln_gamma, ln_beta))
        kh = _split_heads(_layernorm(k @ wk, ln_gamma, ln_beta))
        vh = _split_heads(_layernorm(v @ wv, ln_gamma, ln_beta))
        q_prime = jax.nn.relu(qh) + EPS_K
        k_prime = (jax.nn.relu(kh) + EPS_K) * em
        vh = vh * em
        kv = jnp.einsum('bhnd,bhne->bhde', k_prime, vh)
        z = 1.0 / (jnp.einsum('bhnd,bhd->bhn', q_prime, k_prime.sum(axis=-2)) + EPS_K)
        att = jnp.einsum('bhnd,bhde,bhn->bhne', q_prime, kv, z)
        att = att.reshape(bsz, -1, D_MODEL)
        out = att @ dense_w + dense_b
        return _layernorm(out, ln_gamma, ln_beta)

    def _L0_ffn_ref(x, w_gate, w_up, w_down):
        import jax, jax.numpy as jnp
        import numpy as np
        BLOCK = 32
        W_BITS = 4
        ACT_BITS = 16

        def act_qdq(x):
            qmax = 2.0 ** (ACT_BITS - 1) - 1.0
            scale = jnp.maximum(jnp.max(jnp.abs(x)) / qmax, 1e-12)
            return jnp.clip(jnp.round(x / scale), -qmax - 1.0, qmax) * scale

        def fixed_qdq_u16(x):
            scale = 1.0 / 65536.0
            return jnp.clip(jnp.round(x / scale), 0.0, 65535.0) * scale

        def lpbq_dequant(w):
            O, I = w.shape
            qmax = 2.0 ** (W_BITS - 1) - 1.0
            wb = w.reshape(O, I // BLOCK, BLOCK)
            s = jnp.maximum(jnp.max(jnp.abs(wb), axis=-1, keepdims=True) / qmax, 1e-12)
            wq = jnp.clip(jnp.round(wb / s), -qmax - 1.0, qmax) * s
            return wq.reshape(O, I)
        x = act_qdq(x)
        up = act_qdq(x @ lpbq_dequant(w_up).T)
        gate = act_qdq(x @ lpbq_dequant(w_gate).T)
        sig = fixed_qdq_u16(jax.nn.sigmoid(gate))
        gate = act_qdq(gate * sig)
        o = act_qdq(gate * up)
        return o @ lpbq_dequant(w_down).T

    def _L1_attn_ref(hidden_states, W_attn, b_attn, W_proj, b_proj):
        import jax, jax.numpy as jnp
        import numpy as np
        H = 16
        B, S, E = hidden_states.shape
        hd = E // H
        qkv = hidden_states @ W_attn + b_attn
        qkv = qkv.reshape(B, S, H, 3 * hd).transpose(0, 2, 1, 3)
        q, k, v = jnp.split(qkv, 3, axis=-1)
        scores = jnp.einsum('bhqd,bhkd->bhqk', q, k) / jnp.asarray(hd, q.dtype) ** 0.5
        causal = jnp.tril(jnp.ones((S, S), dtype=bool))
        scores = jnp.where(causal, scores, jnp.asarray(-10000.0, scores.dtype))
        attn_weights = jax.nn.softmax(scores, axis=-1)
        attn_out = jnp.einsum('bhqk,bhkd->bhqd', attn_weights, v)
        attn_out = attn_out.transpose(0, 2, 1, 3).reshape(B, S, E)
        return attn_out @ W_proj + b_proj

    def _L1_xattn_ref(hidden_states, decoder_hidden_states, Wq, Wkv):
        import jax, jax.numpy as jnp
        import numpy as np
        EMBED_DIM = 256
        B, QL, KL = (4, 512, 512)
        d = Wq.shape[0]
        scale = 1.0 / np.sqrt(d)
        query = hidden_states @ Wq
        kv = decoder_hidden_states @ Wkv
        key, value = jnp.split(kv, 2, axis=-1)
        scores = jnp.einsum('bqd,bkd->bqk', query, key) * scale
        w = jax.nn.softmax(scores, axis=-1)
        return jnp.einsum('bqk,bkd->bqd', w, value)

    def _L1_ffn_ref(x, router_w, router_b, expert_w, expert_b):
        import jax, jax.numpy as jnp
        import numpy as np
        EMBED_DIM = 256
        NUM_EXPERTS = 8
        B, S = (2, 512)
        Bb, Ss, D = x.shape
        xt = x.reshape(-1, D)
        logits = xt @ router_w.T + router_b
        probs = jax.nn.softmax(logits, axis=-1)
        idx = jnp.argmax(logits, axis=-1)
        w = jnp.take_along_axis(probs, idx[:, None], axis=1)[:, 0]
        y_all = jnp.einsum('td,efd->tef', xt, expert_w) + expert_b
        y = jnp.take_along_axis(y_all, idx[:, None, None], axis=1)[:, 0]
        out = (y * w[:, None]).reshape(Bb, Ss, D)
        return out
    x = x + _L0_attn_ref(_layernorm(x, axis=-1), L0_attn_qkv_w, L0_attn_qkv_b, L0_attn_out_w, L0_attn_out_b)
    x = x + _L0_xattn_ref(_layernorm(x, axis=-1), ctx_1024, ctx_1024, mask_BxS2_ff1, L0_xattn_wq, L0_xattn_wk, L0_xattn_wv, L0_xattn_ln_gamma, L0_xattn_ln_beta, L0_xattn_dense_w, L0_xattn_dense_b)
    x = x + _L0_ffn_ref(_layernorm(x, axis=-1), L0_ffn_w_gate, L0_ffn_w_up, L0_ffn_w_down)
    x = x + _L1_attn_ref(_layernorm(x, axis=-1), L1_attn_W_attn, L1_attn_b_attn, L1_attn_W_proj, L1_attn_b_proj)
    x = x + _L1_xattn_ref(_layernorm(x, axis=-1), ctx_1024, L1_xattn_Wq, L1_xattn_Wkv)
    x = x + _L1_ffn_ref(_layernorm(x, axis=-1), L1_ffn_router_w, L1_ffn_router_b, L1_ffn_expert_w, L1_ffn_expert_b)
    return x

_drawn_inputs = setup_inputs


def setup_inputs(seed=0):
    import zlib

    import numpy as np

    out = dict(_drawn_inputs(seed))
    spreads = {'L0_attn_qkv_b': (0.0, 0.1),
     'L0_attn_out_b': (0.0, 0.1),
     'L0_xattn_ln_gamma': (1.0, 0.2),
     'L0_xattn_ln_beta': (0.0, 0.1),
     'L0_xattn_dense_b': (0.0, 0.1),
     'L1_attn_b_attn': (0.0, 0.276),
     'L1_attn_b_proj': (0.0, 0.1),
     'L1_ffn_router_b': (0.0, 0.1),
     'L1_ffn_expert_b': (0.0, 0.331)}
    factors = {'L0_attn_qkv_w': 6.938}
    for name, (base, spread) in spreads.items():
        noise = np.random.default_rng([zlib.crc32(name.encode()), seed]).standard_normal(out[name].shape)
        drawn = base * np.exp(spread * noise) if base else spread * noise
        out[name] = jnp.asarray(drawn.astype(out[name].dtype))
    for name, factor in factors.items():
        out[name] = (out[name] * factor).astype(out[name].dtype)
    return out
```

```python
from contextlib import ExitStack

import numpy as np

import concourse.bass as bass
from concourse import mybir

F32 = mybir.dt.float32
F32R = mybir.dt.float32r
BF16 = mybir.dt.bfloat16
I16 = mybir.dt.int16
U16 = mybir.dt.uint16
ALU = mybir.AluOpType
ACT = mybir.ActivationFunctionType
AX = mybir.AxisListType.X

P = 128
B, S, D = 2, 1024, 256
H, HD = 16, 16
T = B * S // P
GT = 4
G = T // GT
GN = GT * P
K = D // P
C = 77
FF = 768
FM = FF // P
QB = 32
E = 8
NK = S // P
HPF = P // HD
PARTS = 4
PROD = PARTS * HD
STK = 96
STKM = 128
SLOTS = 4
VW = 2 * HD
LEAD = 15
RSTD = {"q0": 0, "x0": 1, "f0": 2, "q1": 3, "x1": 4, "m1": 5}
TURN = {"q0": 0, "x0": 1, "q1": 2, "x1": 3, "m1": 4}
NEG = -1e30
W_REST = 15
LN_EPS = 1e-5
X_EPS = 1e-6
QMAX = 32767.0
TINY = 1e-12


class Steps:

    def __init__(self, eng, sem):
        self.eng, self.sem, self.n = eng, sem, 0

    def __call__(self, ins):
        self.n += 1
        ins.then_inc(self.sem, 1)

    def sync(self):
        self.eng.wait_ge(self.sem, self.n)


def causal_width(kb):
    return S - P * kb


def build(nc, d, out):
    ctx = ExitStack()
    with ctx:
        def sb(name, shape, dt=F32):
            return ctx.enter_context(nc.sbuf_tensor(name, shape, dt))

        made = {}

        def sem(name):
            if name not in made:
                made[name] = ctx.enter_context(nc.semaphore(name))
            return made[name]

        x = sb("x", [P, T, D])
        xx = sb("xx", [P, 2 * K * GN * 2])
        xn = xx[:, 0:2 * GT * D].rearrange("p (s t n) -> p s t n", s=2, t=GT)
        xT = xx[:, 2 * GT * D:].rearrange("p (s k n) -> p s k n", s=2, k=K)
        xqT = xx[:, :].rearrange("p (k n) -> p k n", k=K)
        ident = sb("ident", [P, P])
        identb = sb("identb", [P, P], BF16)
        causal = sb("causal", [P, 2, P], BF16)
        stats = sb("stats", [P, GT, 6])
        mv = sb("mv", [P, T, 2])
        veps = sb("veps", [P, T])
        rstd = sb("rstd", [P, T])
        mhalf = sb("mhalf", [P, T])
        ones = sb("ones", [P, P])
        bqk = [sb(f"bqk{i}", [P, 2 * K]) for i in range(2)]
        mask = sb("mask", [C, B])
        gcol = sb("gcol", [P, K])
        bcol = sb("bcol", [P, K])
        rw = sb("rw", [P, K, E])
        rb = sb("rb", [P, E])
        rank = sb("rank", [P, E])
        eb = sb("eb", [E, D])
        km = sb("km", [P, B, K, C])
        v1 = sb("v1", [C, B, D])
        pick = sb("pick", [B * H, B, D])
        qstat = sb("qstat", [P, GT, 6])
        qmv = sb("qmv", [P, 2 * GT, 2])
        qve = sb("qve", [P, 2 * GT])
        qrs = sb("qrs", [P, 2 * GT])
        tin = sb("tin", [P, 2 * NK])
        trow = sb("trow", [2 * NK, P])
        nmax = sb("nmax", [P, 2, NK])
        qs = sb("qs", [P, SLOTS, S], F32R)
        ks = sb("ks", [P, SLOTS, S], F32R)
        xhl = sb("xhl", [P, 2, 2, K, GN], F32R)
        hl = xhl[:, 0, :, :, :]
        am = sb("am", [P, 4 * G * FM])
        sc = sb("sc", [P, 40])

        BIG, WTS = 24576, 4608
        arena = sb("arena", [P, BIG + WTS])

        def at(off, n, *shape, dt=F32):
            v = arena[:, off:off + n]
            if dt != F32:
                v = v.bitcast(dt)
            names = "abcde"[:len(shape)]
            if len(shape) > 1:
                v = v.rearrange(f"p ({' '.join(names)}) -> p {' '.join(names)}", **dict(zip(names[:-1], shape)))
            return v

        vall = at(0, 4096, B, H, NK, HD)
        probs = at(4096, 4096, 4, S)
        osb = at(8192, 1024, SLOTS, 2 * P)
        vs = at(9216, SLOTS * NK * VW, SLOTS, NK, VW)
        num = at(12288, 4096, B, K, S)
        den = at(16384, 1024, S)
        wqk = at(BIG, 1024, K, 2 * D)
        wv = at(BIG + 1024, 512, K, D)
        wo = at(BIG + 1536, 512, K, D)
        bv = at(BIG + 2048, 256, D)
        bo = at(BIG + 2304, 256, D)
        wswap = at(12288, 1024, K, 2 * D)
        cosr = at(13312, 512, 2 * D)
        sinr = at(13824, 512, 2 * D)
        bswap = at(14336, 4, 4)
        coscol = at(14340, 4, 4)
        sincol = at(14344, 4, 4)
        ctxT = at(14352, K * B * C, K, B * C)
        xwkv = at(14720, 1024, K, 2 * D)
        w1q = at(15744, 512, K, D)
        w1kv = at(16256, 1024, K, 2 * D)
        dmask = at(17280, K * (D + H), K, D + H)
        kvn = at(17824, 1024, B, 2 * D)
        vext = at(18848, B * (D + H), B, D + H)
        k1T = at(19392, K * B * C, K, B * C)
        xwq = at(20608, 512, K, D)
        xwd = at(21120, 512, K, D)
        gB = at(21632, 256, D)
        bB = at(21888, 256, D)
        bd = at(22144, 256, D)
        kvbd = at(22400, B * K * (D + H), B, K, D + H)
        qn = at(12288, 2048, 2, GT, D)
        qT = at(14336, 2048, K, S)
        att = at(16384, 2048, NK, D)
        attT = at(18432, 1024, K, GN)
        yb = at(19456, 1024, GT, D)
        zden = at(20480, 64, 64)
        pm = at(12288, GT * C + 4, GT * C + 4)
        pT = at(12672, GN, GN)
        we = at(17408, K * E * D, K, E * D)
        wehl = [st[:, :, :].rearrange("p s n -> p (s n)").rearrange("p (k n) -> p k n", k=K) for st in (qs, ks)]
        x32 = at(13312, 2 * K * GN, 2, K, GN)
        best = at(12960, 2 * GT * E, 2, GT, E)
        raw = at(0, WTS, 144, QB)
        rawg = at(0, FM * D, FM, D)
        rawu = at(FM * D, FM * D, FM, D)
        rawd = at(2 * FM * D, K * FF, K, FF)
        wint = at(WTS, WTS // 2, 144, QB, dt=I16)
        wsc = at(WTS + WTS // 2, 144, 144)
        wrc = at(WTS + WTS // 2 + 144, 144, 144)
        wgT = at(BIG, K * FF, K, FF)
        wuT = at(BIG + K * FF, K * FF, K, FF)
        wdT = at(BIG + 2 * K * FF, FM * D, FM, D)
        act = at(0, FM * T * P, FM, T * P)
        qup = at(12288, FM * T * P // 2, FM, T * P, dt=I16)
        qgate = at(12288 + 6144, FM * T * P // 2, FM, T * P, dt=I16)
        xq = at(12288, T * D, T, D)
        zint = xx[:, :].bitcast(U16).rearrange("p (s n) -> p s n", s=4)

        psum = ctx.enter_context(nc.psum_tensor("psum", [P, 8, 512], F32))
        pflat = psum[:, :, :].rearrange("p b n -> p (b n)")

        lg = at(12288, GT * E, GT, E)
        ex = at(12320, GT * E, GT, E)
        mw = at(12352, GT * E, GT, E)
        lm = at(12384, GT, GT)
        mwT = at(12416, GN, GN)

        qd = nc.dram_tensor("qd", (B * H, 3 * HD, S), F32).ap()
        kd = nc.dram_tensor("kd", (B * H, 2 * HD, S), F32).ap()
        od = nc.dram_tensor("od", (B * H, HD + 1, S), F32).ap()

        block = ctx.enter_context(nc.Block())

        def qunits(g):
            return [(6 * g + u, u) for u in range(6)]

        def a_cols(layer, qt):
            return S if layer == 0 else P * (qt + 1)

        def b_units(layer, kb):
            lo = 0 if layer == 0 else P * kb
            return [(max(lo, a), a + 512) for a in (0, 512) if lo < a + 512]

        def b_before(layer, kb):
            return sum(len(b_units(layer, i)) for i in range(kb))

        def pv_blocks(layer, kb, j):
            return [q for q in (j, NK - 1 - j) if layer == 0 or q >= kb]

        @block.sync
        def _(sp):
            def load(dst, src, name):
                sp.dma_start(dst, src).then_inc(sem(name), 16)

            for g in range(G):
                load(x[:, GT * g:GT * g + GT, :], d["x"][:, GT * g:GT * g + GT, :], f"x_loaded{g}")
            load(ident[:, :], d["ident"], "const_loaded")
            load(wqk, d["wqk0"], "w_qkv0")
            load(wswap, d["wqks"], "w_qkv0")
            load(cosr, d["cos"], "w_qkv0")
            load(sinr, d["sin"], "w_qkv0")
            load(bqk[0][:, :], d["bqk0"], "w_qkv0")
            load(bswap, d["bqks"], "w_qkv0")
            load(coscol, d["coscol"], "w_qkv0")
            load(sincol, d["sincol"], "w_qkv0")
            load(wv, d["wv0"], "w_qkv0")
            load(bv, d["bv0"].partition_broadcast(P), "w_qkv0")
            load(ctxT, d["ctxT"], "w_ctx")
            load(xwkv, d["xwkv"], "w_ctx")
            load(w1kv, d["w1kv"], "w_ctx")
            load(w1q, d["w1q"], "w_ctx")
            load(mask[:, :], d["mask"], "w_ctx")
            load(gB[:, :], d["g"].partition_broadcast(P), "w_ctx")
            load(bB[:, :], d["b"].partition_broadcast(P), "w_ctx")
            load(dmask, d["dmask"], "w_ctx")
            load(wo, d["wo0"], "w_rest")
            load(bo, d["bo0"].partition_broadcast(P), "w_rest")
            load(xwq[:, :, :], d["xwq"], "w_rest")
            load(xwd[:, :, :], d["xwd"], "w_rest")
            load(bd[:, :], d["bd"].partition_broadcast(P), "w_rest")
            load(gcol[:, :], d["gcol"], "w_rest")
            load(bcol[:, :], d["bcol"], "w_rest")
            load(bqk[1][:, :], d["bqk1"], "w_rest")
            load(rw[:, :, :], d["rw"], "w_rest")
            load(rb[:, :], d["rb"].partition_broadcast(P), "w_rest")
            load(eb[:, :], d["eb"], "w_rest")
            load(rank[:, :], d["rank"], "w_rest")
            load(causal[:, :, :], d["causal"], "w_rest")
            load(pick[:, :, :], d["pick"], "w_rest")
            load(identb[:, :], d["identb"], "w_rest")

            def store_split(layer):
                for g in range(G):
                    b, c0 = divmod(g * GN, S)
                    for n, u in qunits(g)[:4]:
                        is_q, ft = u < K, u % K
                        sp.wait_ge(sem("qkv_drained"), 6 * G * layer + n + 1)
                        h0 = b * H + ft * HPF
                        for part, src in enumerate((0, 1, 0) if is_q else (0, 1)):
                            dst = (qd if is_q else kd)[h0:h0 + HPF, HD * part:HD * part + HD, c0:c0 + GN]
                            sp.dma_start(dst, hl[:, u % 2, src, :].bitcast(F32)).then_inc(sem(f"split_stored{layer}_{u}"), 16)
                for u in range(4):
                    sp.wait_ge(sem(f"split_stored{layer}_{u}"), 16 * G * (3 if u < K else 2))

            def attention(layer):
                def load_stack(s, bh):
                    loaded = sem(f"stack_loaded{layer}_{s}")
                    sp.dma_start(qs[0:2 * HD, s, :].bitcast(F32), qd[bh, 0:2 * HD, :]).then_inc(loaded, 16)
                    sp.dma_start(qs[2 * HD:4 * HD, s, :].bitcast(F32), qd[bh, HD:3 * HD, :]).then_inc(loaded, 16)
                    sp.dma_start(ks[0:2 * HD, s, :].bitcast(F32), kd[bh, :, :]).then_inc(loaded, 16)
                    sp.dma_start(ks[2 * HD:4 * HD, s, :].bitcast(F32), kd[bh, :, :]).then_inc(loaded, 16)

                def load_max(s, head):
                    sp.wait_ge(sem("max_rows"), B * H * layer + head + 1)
                    for part in range(2):
                        sp.dma_start(qs[STK + part:STK + part + 1, s, :].bitcast(F32).rearrange("p (t c) -> p t c", t=NK),
                                     trow[NK * part:NK * part + NK, :]).then_inc(sem(f"max_loaded{layer}_{s}"), 16)

                for s in range(SLOTS):
                    load_stack(s, s)
                load_max(0, 0)

                def heads(i, last):
                    for s in range(SLOTS):
                        head = SLOTS * i + s
                        if not (last and s == SLOTS - 1):
                            load_max((s + 1) % SLOTS, head + 1)
                        if not last:
                            sp.wait_ge(sem(f"scores{layer}"), b_before(layer, NK) * (head + 1))
                            load_stack(s, head + SLOTS)

                with sp.Fori(0, B * H // SLOTS - 1) as i:
                    heads(i, False)
                heads(B * H // SLOTS - 1, True)

            def load_attended(layer):
                for s in range(SLOTS):
                    sp.wait_ge(sem(f"out_stored{layer}_{s}"), 64 * (B * H // SLOTS))
                load(den[0:B * H, :], od[:, HD, :], f"sums_loaded{layer}")
                for b in range(B):
                    for k in range(K):
                        h0 = b * H + k * HPF
                        load(num[:, b, k, :], od[h0:h0 + HPF, 0:HD, :], f"attended_loaded{layer}_{b}")

            store_split(0)
            attention(0)
            load_attended(0)
            load(at(0, WTS), d["ffw"], "w_ffn")
            sp.wait_ge(sem("down_mm"), 2 * G)
            load(wqk, d["wqk1"], "w_qkv1")
            load(wv, d["wv1"], "w_qkv1")
            load(bv, d["bv1"].partition_broadcast(P), "w_qkv1")
            load(wo, d["wo1"], "w_qkv1")
            load(bo, d["bo1"].partition_broadcast(P), "w_qkv1")
            store_split(1)
            attention(1)
            load_attended(1)
            load(we, d["we"], "w_experts")
            for g in range(G):
                sp.wait_ge(sem("moe_done"), g + 1)
                sp.dma_start(out[:, GT * g:GT * g + GT, :], x[:, GT * g:GT * g + GT, :]).then_inc(sem("out_stored"), 16)
            sp.wait_ge(sem("out_stored"), 16 * G)

        def bc(ap, n, axis=1):
            shape = list(ap.shape)
            shape.insert(axis, n)
            return ap.unsqueeze(axis).broadcast_to(shape)

        @block.gpsimd
        def _(gp):
            gp.memset(mhalf[:, :], -0.5).then_inc(sem("pool_const"), 1)
            gp.memset(ones[:, :], 1.0).then_inc(sem("pool_const"), 1)
            gp.wait_ge(sem("pool_const"), 2)

            def power(dst, src, need, n, done):
                gp.wait_ge(sem(need), n)
                gp.tensor_tensor(dst, src, mhalf[0:dst.shape[0], 0:dst.shape[1]], ALU.pow).then_inc(sem(done), 1)

            def rstd_groups(tag, g):
                power(rstd[:, GT * g:GT * g + GT], veps[:, GT * g:GT * g + GT], "var_ready", G * RSTD[tag] + g + 1, "rstd_ready")

            def add_rows(g, row, done):
                for t in range(GT * g, GT * g + GT):
                    ins = gp.tensor_tensor(x[:, t, :], x[:, t, :], row, ALU.add)
                ins.then_inc(sem(done), 1)

            def attention(layer):
                vheads = at(0, 4096, B * H, NK, HD)

                def copy_values(s, bh):
                    gp.tensor_copy(vs[:, s, :, 0:HD], vheads[:, bh, :, :]).then_inc(sem("values_copied"), 1)

                def store_out(s, head):
                    gp.wait_ge(sem(f"out_ready{layer}"), head + 3)
                    for j in range(4):
                        dst = od[head, :, :].rearrange("r (q c) -> r q c", q=NK)[:, j:NK - j:NK - 1 - 2 * j, :]
                        src = osb[32 * j:32 * j + HD + 1, s, :].rearrange("r (q c) -> r q c", q=2)
                        gp.dma_start(dst, src).then_inc(sem(f"out_stored{layer}_{s}"), 16)

                gp.wait_ge(sem("qkv_drained"), 6 * G * layer + 6 * G)
                for s in range(SLOTS):
                    copy_values(s, s)
                gp.wait_ge(sem("w_rest" if layer == 0 else "w_qkv1"), 16 * (W_REST if layer == 0 else 5))
                for g in range(G):
                    add_rows(g, bo, "bias_added")
                with gp.Fori(0, B * H // SLOTS - 1) as i:
                    for s in range(SLOTS):
                        store_out(s, SLOTS * i + s)
                        copy_values(s, SLOTS * i + s + SLOTS)
                for s in range(SLOTS):
                    store_out(s, B * H - SLOTS + s)

            power(qrs[0:C, 0:4], qve[0:C, 0:4], "ctx_var", 1, "ctx_rstd")
            for g in range(G):
                rstd_groups("q0", g)
            gp.wait_ge(sem("rstd_ready"), G)
            for n, stack in enumerate((qs, ks)):
                gp.memset(stack[PROD:STKM, :, :].bitcast(F32), 0.0).then_inc(sem("stack_zeros"), 1)
                gp.wait_ge(sem("stack_zeros"), n + 1)
            gp.memset(ks[STK:STK + 2, :, :].bitcast(F32), 1.0).then_inc(sem("stack_ones"), 1)
            gp.wait_ge(sem("stack_ones"), 1)
            attention(0)
            for g in range(G):
                rstd_groups("x0", g)

            def cross0_power(g, which):
                lo = GT * which
                power(qrs[:, lo:lo + GT], qve[:, lo:lo + GT], f"x0_var{which}", g + 1, f"x0_rstd{which}")

            gp.wait_ge(sem("xn_ready"), G * TURN["x0"] + 1)
            add_rows(0, bB[:, :], "beta_added")
            cross0_power(0, 0)
            for g in range(G):
                if g + 1 < G:
                    cross0_power(g + 1, 0)
                    gp.wait_ge(sem("xn_ready"), G * TURN["x0"] + g + 2)
                    add_rows(g + 1, bB[:, :], "beta_added")
                for gg in (g - 1, g) if g % 2 else ():
                    cross0_power(gg, 1)
                    rstd_groups("f0", gg)
            for g in range(G):
                rstd_groups("q1", g)
            attention(1)
            for g in range(G):
                rstd_groups("x1", g)
            gp.wait_ge(sem("we_high"), 1)
            gp.tensor_tensor(wehl[1], we, wehl[0].bitcast(F32), ALU.subtract).then_inc(sem("we_low"), 1)
            for g in range(G):
                rstd_groups("m1", g)

        @block.scalar
        def _(sc_):
            act_ = nc.scalar.activation

            def evac_T(tag, g, free=None):
                sc_.wait_ge(sem("lnT"), G * TURN[tag] + g + 1)
                if free and g >= 2:
                    sc_.wait_ge(sem(free[0]), free[1](g - 2))
                for k in range(K):
                    ins = act_(xT[:, g % 2, k, :], psum[:, k, :], ACT.Copy)
                ins.then_inc(sem("xT_ready"), 1)

            sc_.wait_ge(sem("ctx_mm"), 1)
            for b in range(B):
                act_(v1[:, b, :], psum[0:C, 2 + b, 0:D], ACT.Copy)
            for m in range(K):
                ins = act_(k1T[:, m, :], psum[:, 4 + m, 0:B * C], ACT.Copy)
            ins.then_inc(sem("k1T_ready"), 1)
            sc_.wait_ge(sem("km_mm"), 1)
            for b in range(B):
                for m in range(K):
                    ins = act_(km[:, b, m, :], psum[:, 6 + m, C * b:C * b + C], ACT.Copy)
            ins.then_inc(sem("km_ready"), 1)

            def qkv(layer):
                tag = f"q{layer}"
                for g in range(G):
                    if g == 0:
                        evac_T(tag, 0)
                    if g + 1 < G:
                        evac_T(tag, g + 1, ("qkv_mm", lambda p: 6 * (G * layer + p + 1)))
                    for n, u in qunits(g)[:4]:
                        sc_.wait_ge(sem("qkv_mm"), 6 * G * layer + n + 1)
                        if u >= 2:
                            sc_.wait_ge(sem(f"split_stored{layer}_{u - 2}"), 48 * (g + 1))
                        elif g >= 1:
                            sc_.wait_ge(sem(f"split_stored{layer}_{u + 2}"), 32 * g)
                        act_(hl[:, u % 2, 0, :], psum[:, 4 + n % 4, :], ACT.Identity,
                             bias=bqk[layer][:, u:u + 1]).then_inc(sem("high_ready"), 1)

            def attention(layer):
                per = b_before(layer, NK)
                sc_.sem_inc(sem(f"probs_ready{layer}"), 2)
                sc_.sem_inc(sem(f"out_ready{layer}"), 2)

                def exps(head, kb):
                    sc_.wait_ge(sem(f"pv{layer}"), NK * head + kb + 1)
                    for r, (lo, hi) in enumerate(b_units(layer, kb)):
                        idx = b_before(layer, kb) + r
                        sc_.wait_ge(sem(f"scores{layer}"), per * head + idx + 1)
                        act_(probs[:, kb % 4, lo:hi], psum[:, 4 + idx % 2, lo % 512:lo % 512 + hi - lo], ACT.Exp,
                             scale=HD ** -0.5).then_inc(sem(f"probs_ready{layer}"), 1)

                def heads(i, first, last):
                    for s in range(SLOTS):
                        head = SLOTS * i + s
                        for t in range(NK):
                            if t + 1 < NK:
                                exps(head, t + 1)
                            elif not (last and s == SLOTS - 1):
                                exps(head + 1, 0)
                        sc_.wait_ge(sem(f"pv{layer}"), NK * (head + 1) + 4)
                        if not first:
                            sc_.wait_ge(sem(f"out_stored{layer}_{s}"), 64 * i)
                        act_(osb[:, s, :], psum[:, 6 + s % 2, 0:2 * P], ACT.Copy).then_inc(sem(f"out_ready{layer}"), 1)

                exps(0, 0)
                heads(0, True, False)
                with sc_.Fori(1, B * H // SLOTS - 1) as i:
                    heads(i, False, False)
                heads(B * H // SLOTS - 1, False, True)

            def ffn_weights():
                for n in range(9):
                    sc_.wait_ge(sem("wT_mm"), n + 1)
                    act_(at(BIG + 512 * n, 512), psum[:, n % 4, :], ACT.Copy).then_inc(sem("wT_ready"), 1)

            def cross0():
                def rest(g):
                    sc_.wait_ge(sem("x0_T2"), g + 1)
                    for k in range(K):
                        ins = act_(qT[:, k, GN * (g % 2):GN * (g % 2) + GN], psum[:, 4 + k, :], ACT.Identity, scale=gcol[:, k:k + 1], bias=bcol[:, k:k + 1])
                    ins.then_inc(sem("x0_affine"), 1)
                evac_T("x0", 0)
                for g in range(G):
                    if g + 1 < G:
                        evac_T("x0", g + 1, ("x0_q", lambda p: p + 1))
                    rest(g)
                    for gg in (g - 1, g) if g % 2 else ():
                        sc_.wait_ge(sem("x0_T3"), gg + 1)
                        for k in range(K):
                            ins = act_(attT[:, k, :], psum[:, 4 + k, :], ACT.Copy)
                        ins.then_inc(sem("x0_attT"), 1)

            def ffn():
                for g in range(G):
                    sc_.wait_ge(sem("f_T"), g + 1)
                    for k in range(K):
                        ins = act_(xqT[:, k, GN * g:GN * g + GN], psum[:, 2 * (g % 2) + k, :], ACT.Copy)
                    ins.then_inc(sem("xqT_ready"), 1)
                for n in range(2 * FM * G):
                    m, g = divmod(n % (FM * G), G)
                    sc_.wait_ge(sem("f_mm"), n + 1)
                    if n >= FM * G:
                        sc_.wait_ge(sem("qup_ready"), m + 1)
                    act_(act[:, m, GN * g:GN * g + GN], psum[:, n % 6, :], ACT.Copy).then_inc(sem("f_evac"), 1)
                for m in range(FM):
                    sc_.wait_ge(sem("qgate_ready"), m + 1)
                    act_(act[:, m, :], qgate[:, m, :], ACT.Sigmoid, scale=sc[:, 20:21]).then_inc(sem("sigmoid_ready"), 1)
                sc_.wait_ge(sem("p_scaled"), 1)
                for m in range(FM):
                    act_(qgate[:, m, :], act[:, m, :], ACT.Identity, scale=sc[:, 26:27]).then_inc(sem("qp_ready"), 1)

            def cross1():
                sc_.wait_ge(sem("w_experts"), 16)
                sc_.wait_ge(sem("proj_done"), 4 * G)
                act_(wehl[0], we, ACT.Copy).then_inc(sem("we_high"), 1)
                for g in range(G):
                    if g == 0:
                        evac_T("x1", 0)
                    if g + 1 < G:
                        evac_T("x1", g + 1, ("x1_scores", lambda p: p + 1))
                    sc_.wait_ge(sem("x1_max"), g + 1)
                    for t in range(GT):
                        ins = act_(pm[:, C * t:C * t + C], psum[:, 2, C * t:C * t + C], ACT.Exp, scale=D ** -0.5,
                                   bias=qve[:, t:t + 1], accum_out=qrs[:, t:t + 1])
                    ins.then_inc(sem("x1_exp"), 1)
                    sc_.wait_ge(sem("x1_T2"), g + 1)
                    act_(pT[0:C, :], psum[0:C, 3, :], ACT.Copy).then_inc(sem("x1_pT"), 1)

            def experts():
                def turned(g):
                    sc_.wait_ge(sem("lnT"), G * TURN["m1"] + g + 1)
                    if g >= 2:
                        sc_.wait_ge(sem("m1_mm"), 16 * (g - 1))
                    for k in range(K):
                        act_(xhl[:, g % 2, 0, k, :], psum[:, k, :], ACT.Copy)
                    for k in range(K):
                        ins = act_(x32[:, g % 2, k, :], psum[:, k, :], ACT.Copy)
                    ins.then_inc(sem("xT_ready"), 1)

                def routing(g):
                    sc_.wait_ge(sem("m1_shift"), g + 1)
                    act_(ex, ex, ACT.Exp).then_inc(sem("m1_exp"), 1)
                    sc_.wait_ge(sem("m1_T2"), g + 1)
                    act_(mwT[0:E, :], psum[0:E, 3, :], ACT.Copy).then_inc(sem("m1_mwT"), 1)

                turned(0)
                turned(1)
                routing(0)
                for g in range(G):
                    if g + 1 < G:
                        routing(g + 1)
                    if g + 2 < G:
                        turned(g + 2)

            qkv(0)
            attention(0)
            ffn_weights()
            cross0()
            ffn()
            qkv(1)
            attention(1)
            cross1()
            experts()

        @block.tensor
        def _(pe):
            mm = nc.tensor.matmul

            def transpose_rows(tag, g):
                pe.wait_ge(sem("xn_ready"), G * TURN[tag] + g + 1)
                if g >= 1:
                    pe.wait_ge(sem("xT_ready"), G * TURN[tag] + g)
                for k in range(K):
                    for t in range(GT):
                        ins = nc.tensor.transpose(psum[:, k, P * t:P * t + P], xn[:, g % 2, t, P * k:P * k + P], ident[:, :])
                ins.then_inc(sem("lnT"), 1)

            pe.wait_ge(sem("w_ctx"), 16 * 8)
            for b in range(B):
                cols = slice(C * b, C * b + C)
                for k in range(K):
                    mm(psum[0:C, b, :], ctxT[:, k, cols], xwkv[:, k, :], start=(k == 0), stop=(k == K - 1))
                for k in range(K):
                    mm(psum[0:C, 2 + b, 0:D], ctxT[:, k, cols], w1kv[:, k, D:2 * D], start=(k == 0), stop=(k == K - 1))
            for m in range(K):
                for k in range(K):
                    ins = mm(psum[:, 4 + m, 0:B * C], w1kv[:, k, P * m:P * m + P], ctxT[:, k, :], start=(k == 0), stop=(k == K - 1))
            ins.then_inc(sem("ctx_mm"), 1)
            pe.wait_ge(sem("k1T_ready"), 1)
            for m in range(K):
                for k in range(K):
                    ins = mm(psum[:, 6 + m, 0:B * C], w1q[:, k, P * m:P * m + P], k1T[:, k, :], start=(k == 0), stop=(k == K - 1))
            ins.then_inc(sem("km_mm"), 1)
            pe.wait_ge(sem("ctx_kv"), 1)
            for b in range(B):
                for m in range(K):
                    ins = mm(psum[:, 2 * b + m, 0:D + H], kvn[0:C, b, P * m:P * m + P], vext[0:C, b, :], start=True, stop=True)
            ins.then_inc(sem("kv_mm"), 1)
            pe.wait_ge(sem("kvbd_ready"), 1)
            pe.wait_ge(sem("km_ready"), 1)
            pe.wait_ge(sem("const_loaded"), 16)

            def qkv(layer):
                tag = f"q{layer}"
                transpose_rows(tag, 0)
                if layer == 0:
                    pe.wait_ge(sem("w_rotated"), 1)
                else:
                    pe.wait_ge(sem("w_qkv1"), 16 * 5)
                for g in range(G):
                    if g + 1 < G:
                        transpose_rows(tag, g + 1)
                    pe.wait_ge(sem("xT_ready"), G * TURN[tag] + g + 1)
                    for n, u in qunits(g):
                        bank = 4 + n % 4
                        if n >= 4:
                            pe.wait_ge(sem("qkv_drained"), 6 * G * layer + n - 3)
                        if u < 4:
                            for k in range(K):
                                ins = mm(psum[:, bank, :], wqk[:, k, P * u:P * u + P], xT[:, g % 2, k, :],
                                         start=(k == 0), stop=(k == K - 1))
                        else:
                            for i in range(2):
                                t = 2 * (u - 4) + i
                                for k in range(K):
                                    ins = mm(psum[:, bank, D * i:D * i + D], xT[:, g % 2, k, P * t:P * t + P], wv[:, k, :],
                                             start=(k == 0), stop=(k == K - 1))
                        ins.then_inc(sem("qkv_mm"), 1)

            def attention(layer):
                per = b_before(layer, NK)
                pe.wait_ge(sem("ones_ready"), layer + 1)
                pe.sem_inc(sem(f"pv{layer}"), 4)
                if layer == 0:
                    pe.wait_ge(sem("w_rest"), 16 * W_REST)
                    pe.wait_ge(sem("stack_ones"), 1)
                pe.wait_ge(sem("qkv_drained"), 6 * G * layer + 6 * G)

                def max_scores(head, s, use, qt, ring=True):
                    if qt == 0:
                        pe.wait_ge(sem(f"stack_loaded{layer}_{s}"), 64 * use + 64)
                    if ring:
                        pe.wait_ge(sem(f"max_taken{layer}"), NK * head + qt - 1)
                    cols = a_cols(layer, qt)
                    q = qs[0:STK, s, P * qt:P * qt + P]
                    for half in range((cols + 511) // 512):
                        lo, hi = 512 * half, min(cols, 512 * half + 512)
                        diag = layer == 1 and hi == cols
                        bank = 2 * (qt % 2) + half
                        ins = mm(psum[:, bank, 0:hi - lo], q, ks[0:STK, s, lo:hi], start=True, stop=not diag)
                        if diag:
                            ins = mm(psum[:, bank, hi - lo - P:hi - lo], identb[:, :], causal[:, 0, :], start=False, stop=True)
                    ins.then_inc(sem(f"max_scores{layer}"), 1)

                def turn_max(head, par):
                    pe.wait_ge(sem("max_split"), B * H * layer + head + 1)
                    pe.wait_ge(sem(f"out_ready{layer}"), head + 1)
                    nc.tensor.transpose(psum[0:2 * NK, 6 + par, 384:512], tin[:, :], ident[:, :]).then_inc(sem("max_turned"), 1)

                def scores(head, s, use, kb):
                    if kb == 0:
                        pe.wait_ge(sem(f"max_loaded{layer}_{s}"), 32 * use + 32)
                    k = ks[0:STKM, s, P * kb:P * kb + P]
                    for r, (lo, hi) in enumerate(b_units(layer, kb)):
                        idx = b_before(layer, kb) + r
                        pe.wait_ge(sem(f"probs_ready{layer}"), per * head + idx + 1)
                        diag = layer == 1 and r == 0
                        bank, off = 4 + idx % 2, lo % 512
                        ins = mm(psum[:, bank, off:off + hi - lo], k, qs[0:STKM, s, lo:hi], start=True, stop=not diag)
                        if diag:
                            ins = mm(psum[:, bank, off:off + P], identb[:, :], causal[:, 1, :], start=False, stop=True)
                        ins.then_inc(sem(f"scores{layer}"), 1)

                def values(head, s, kb):
                    if kb == 0:
                        pe.wait_ge(sem("values_copied"), B * H * layer + head + 1)
                        pe.wait_ge(sem(f"out_ready{layer}"), head + 1)
                    pe.wait_ge(sem(f"probs_ready{layer}"), per * head + b_before(layer, kb + 1) + 2)
                    for j in range(4):
                        qt = pv_blocks(layer, kb, j)
                        if not qt:
                            continue
                        lo = 0 if len(qt) == 2 else P
                        rhs = probs[:, kb % 4, :].rearrange("p (q c) -> p q c", q=NK)[:, qt[0]:qt[-1] + 1:max(1, qt[-1] - qt[0]), :]
                        dst = psum[32 * j:32 * j + VW, 6 + s % 2, lo:2 * P].rearrange("p (q c) -> p q c", c=P)
                        last = kb == NK - 1 if layer == 0 else kb == NK - 1 - j
                        ins = mm(dst, vs[:, s, kb, :], rhs, start=(kb == 0), stop=last, skip_group_check=True)
                    ins.then_inc(sem(f"pv{layer}"), 1)

                for a in range(LEAD):
                    max_scores(a // NK, a // NK, 0, a % NK, ring=a >= 2)
                    if a == NK + 1:
                        turn_max(0, 0)
                scores(0, 0, 0, 0)

                def heads(i, last):
                    for s in range(SLOTS):
                        head = SLOTS * i + s
                        for t in range(NK):
                            dh, r = divmod(t + LEAD, NK)
                            if not (last and s + dh >= SLOTS):
                                max_scores(head + dh, (s + dh) % SLOTS, i + (s + dh) // SLOTS, r)
                            if t + 1 < NK:
                                scores(head, s, i, t + 1)
                            elif not (last and s == SLOTS - 1):
                                scores(head + 1, (s + 1) % SLOTS, i + (s + 1) // SLOTS, 0)
                            values(head, s, t)
                            if t == 2 and not (last and s == SLOTS - 1):
                                turn_max(head + 1, (s + 1) % 2)

                with pe.Fori(0, B * H // SLOTS - 1) as i:
                    heads(i, False)
                heads(B * H // SLOTS - 1, True)

            def project(layer):
                for n in range(4 * B):
                    b, half, k = n // 4, n // 2 % 2, n % 2
                    pe.wait_ge(sem("sums_inverted"), 4 * layer + (2 * half + 2 if b == 0 else 4))
                    if n >= 4:
                        pe.wait_ge(sem("attn_ready"), 4 * B * layer + n - 3)
                    mm(psum[:, n % 4, :], pick[:, b, P * k:P * k + P], den[0:B * H, 512 * half:512 * half + 512],
                       start=True, stop=True).then_inc(sem("sums_spread"), 1)
                for u in range(2 * G):
                    b = u // G
                    pe.wait_ge(sem("attn_ready"), 4 * B * layer + 2 * (u // 2) + 2)
                    if u >= 4:
                        pe.wait_ge(sem("proj_drained"), 2 * G * layer + u - 3)
                    for i in range(2):
                        kb = (2 * u + i) % NK
                        for k in range(K):
                            ins = mm(psum[:, 4 + u % 4, D * i:D * i + D], num[:, b, k, P * kb:P * kb + P], wo[:, k, :],
                                     start=(k == 0), stop=(k == K - 1))
                    ins.then_inc(sem("proj_done"), 1)

            def ffn_weights():
                pe.wait_ge(sem("w_dequant"), 1)
                for n in range(9):
                    if n >= 4:
                        pe.wait_ge(sem("wT_ready"), n - 3)
                    for c in range(4):
                        i = 4 * (n % 3) + c
                        if n < 6:
                            k, m = divmod(i, FM)
                            src = (rawg if n < 3 else rawu)[:, m, P * k:P * k + P]
                        else:
                            m, k = divmod(i, K)
                            src = rawd[:, k, P * m:P * m + P]
                        ins = nc.tensor.transpose(psum[:, n % 4, P * c:P * c + P], src, ident[:, :])
                    ins.then_inc(sem("wT_mm"), 1)

            def rows_times(g, w, bank, name, src, cols=D):
                for t in range(GT):
                    for k in range(K):
                        ins = mm(psum[:, bank + t // 2, D * (t % 2):D * (t % 2) + cols], src[:, k, P * t:P * t + P], w[:, k, 0:cols],
                                 start=(k == 0), stop=(k == K - 1))
                ins.then_inc(sem(name), 1)

            def cross0():
                pe.wait_ge(sem("wT_ready"), 9)

                def queries(g):
                    pe.wait_ge(sem("xT_ready"), G * TURN["x0"] + g + 1)
                    if g >= 1:
                        pe.wait_ge(sem("x0_qn"), g)
                    rows_times(g, xwq, 2, "x0_q", xT[:, g % 2])

                def turn(src, done):
                    for k in range(K):
                        for t in range(GT):
                            ins = nc.tensor.transpose(psum[:, 4 + k, P * t:P * t + P], src[:, t, P * k:P * k + P], ident[:, :])
                    ins.then_inc(sem(done), 1)

                transpose_rows("x0", 0)
                queries(0)
                for g in range(G):
                    b = g // 2
                    if g + 1 < G:
                        transpose_rows("x0", g + 1)
                    pe.wait_ge(sem("x0_qn"), g + 1)
                    if g >= 2:
                        pe.wait_ge(sem("x0_attT"), 2 * (g // 2))
                    elif g == 1:
                        pe.wait_ge(sem("x0_affine"), 1)
                    if g == 3:
                        pe.wait_ge(sem("x0_affine"), 3)
                    turn(qn[:, g % 2], "x0_T2")
                    if g + 1 < G:
                        queries(g + 1)
                    if g % 2 == 0:
                        continue
                    pe.wait_ge(sem("x0_qT"), g + 1)
                    if b:
                        pe.wait_ge(sem("x0_y"), 2 * b)
                    for half in range(2):
                        if half:
                            pe.wait_ge(sem("x0_att"), 2 * b + 1)
                        for i in range(NK):
                            nn = NK * half + i
                            for j in range(2):
                                for k in range(K):
                                    kv = kvbd[:, b, k, 0:D].rearrange("p (t j e) -> p j t e", j=2, e=HD)[:, j, 4 * k:4 * k + 4, :]
                                    lo = P * (i % 4) + 64 * k
                                    dst = psum[64 * j:64 * j + 64, 6 + i // 4, lo:lo + 64]
                                    mm(dst.rearrange("p (t e) -> p t e", e=HD), qT[:, k, nn:S:HD], kv, start=True, stop=True)
                        for i in range(NK):
                            nn = NK * half + i
                            for j in range(2):
                                for k in range(K):
                                    lo = NK * i + 4 * k
                                    ins = mm(psum[64 * j:64 * j + 64, 4, lo:lo + 4], qT[:, k, nn:S:HD],
                                             kvbd[:, b, k, D:D + H].rearrange("p (t j) -> p j t", j=2)[:, j, 4 * k:4 * k + 4],
                                             start=True, stop=True)
                        ins.then_inc(sem("x0_kv"), 1)
                    pe.wait_ge(sem("x0_att"), 2 * b + 2)
                    for gg in (g - 1, g):
                        if gg % 2:
                            pe.wait_ge(sem("x0_attT"), gg)
                            pe.wait_ge(sem("x0_y"), gg)
                        turn(att[:, GT * (gg % 2):GT * (gg % 2) + GT], "x0_T3")
                        pe.wait_ge(sem("x0_attT"), gg + 1)
                        rows_times(gg, xwd, 6, "x0_out", attT)

            def global_max(n):
                pe.wait_ge(sem("gm_col"), n + 1)
                mm(psum[0:1, 7, 0:P], sc[:, 0:1], ident[:, :], start=True, stop=True).then_inc(sem("gm_row"), 1)
                pe.wait_ge(sem("gm_one"), n + 1)
                mm(psum[:, 7, 256:257], ones[0:1, :], sc[0:1, 1:2], start=True, stop=True).then_inc(sem("gm_all"), 1)

            def ffn():
                global_max(0)
                for g in range(G):
                    pe.wait_ge(sem("xq_ready"), g + 1)
                    if g >= 2:
                        pe.wait_ge(sem("xqT_ready"), g - 1)
                    for k in range(K):
                        for t in range(GT):
                            ins = nc.tensor.transpose(psum[:, 2 * (g % 2) + k, P * t:P * t + P],
                                                      xq[:, GT * g + t, P * k:P * k + P], ident[:, :])
                    ins.then_inc(sem("f_T"), 1)
                pe.wait_ge(sem("xqT_ready"), G)
                for n in range(2 * FM * G):
                    m, g = divmod(n % (FM * G), G)
                    if n >= 6:
                        pe.wait_ge(sem("f_evac"), n - 5)
                    if n == FM * G + 4:
                        global_max(1)
                    w = wuT if n < FM * G else wgT
                    for k in range(K):
                        ins = mm(psum[:, n % 6, :], w[:, k, P * m:P * m + P], xqT[:, k, GN * g:GN * g + GN],
                                 start=(k == 0), stop=(k == K - 1))
                    ins.then_inc(sem("f_mm"), 1)
                for n in (2, 3, 4):
                    global_max(n)
                for u in range(2 * G):
                    pe.wait_ge(sem("q3_ready"), u // 2 + 1)
                    if u >= 4:
                        pe.wait_ge(sem("down_drained"), u - 3)
                    for i in range(2):
                        t = 2 * u + i
                        for m in range(FM):
                            ins = mm(psum[:, u % 4, D * i:D * i + D], act[:, m, P * t:P * t + P], wdT[:, m, :],
                                     start=(m == 0), stop=(m == FM - 1))
                    ins.then_inc(sem("down_mm"), 1)

            def cross1():
                transpose_rows("x1", 0)
                for g in range(G):
                    b = g // 2
                    if g + 1 < G:
                        transpose_rows("x1", g + 1)
                    pe.wait_ge(sem("xT_ready"), G * TURN["x1"] + g + 1)
                    if g >= 1:
                        pe.wait_ge(sem("x1_exp"), g)
                    for t in range(GT):
                        for k in range(K):
                            ins = mm(psum[:, 2, C * t:C * t + C], xT[:, g % 2, k, P * t:P * t + P], km[:, b, k, :],
                                     start=(k == 0), stop=(k == K - 1))
                    ins.then_inc(sem("x1_scores"), 1)
                    pe.wait_ge(sem("x1_exp"), g + 1)
                    if g >= 1:
                        pe.wait_ge(sem("x1_pT"), g)
                    for t in range(GT):
                        ins = nc.tensor.transpose(psum[0:C, 3, P * t:P * t + P], pm[:, C * t:C * t + C], ident[:, :])
                    ins.then_inc(sem("x1_T2"), 1)
                    pe.wait_ge(sem("x1_pT"), g + 1)
                    if g >= 1:
                        pe.wait_ge(sem("x1_added"), g)
                    for t in range(GT):
                        ins = mm(psum[:, 6 + t // 2, D * (t % 2):D * (t % 2) + D], pT[0:C, P * t:P * t + P], v1[0:C, b, :],
                                 start=True, stop=True)
                    ins.then_inc(sem("x1_out"), 1)

            def experts():
                def logits(g):
                    pe.wait_ge(sem("xT_ready"), G * TURN["m1"] + g + 1)
                    for t in range(GT):
                        for k in range(K):
                            ins = mm(psum[:, 2, E * t:E * t + E], x32[:, g % 2, k, P * t:P * t + P], rw[:, k, :],
                                     start=(k == 0), stop=(k == K - 1))
                    ins.then_inc(sem("m1_logits"), 1)

                def weights_to_rows(g):
                    pe.wait_ge(sem("m1_mw"), g + 1)
                    for t in range(GT):
                        ins = nc.tensor.transpose(psum[0:E, 3, P * t:P * t + P], mw[:, t, :], ident[:, :])
                    ins.then_inc(sem("m1_T2"), 1)

                def bias(g):
                    pe.wait_ge(sem("m1_mwT"), g + 1)
                    for t in range(GT):
                        ins = mm(psum[:, 2 + t // 2, D * (t % 2):D * (t % 2) + D], mwT[0:E, P * t:P * t + P], eb[:, :],
                                 start=True, stop=True)
                    ins.then_inc(sem("m1_bias"), 1)

                def expert_pairs(g, t):
                    for c in range(E // 2):
                        n = 16 * g + 4 * t + c
                        if n >= 4:
                            pe.wait_ge(sem("m1_added"), n - 3)
                        cols = slice(2 * D * c, 2 * D * c + 2 * D)
                        rows = slice(P * t, P * t + P)
                        terms = [(k, xp, wp) for k in range(K) for xp, wp in ((0, 0), (0, 1), (1, 0))]
                        for i, (k, xp, wp) in enumerate(terms):
                            ins = mm(psum[:, 4 + n % 4, :], xhl[:, g % 2, xp, k, rows], wehl[wp][:, k, cols],
                                     start=(i == 0), stop=(i == len(terms) - 1))
                        ins.then_inc(sem("m1_mm"), 1)

                transpose_rows("m1", 0)
                logits(0)
                pe.wait_ge(sem("m1_low"), 1)
                transpose_rows("m1", 1)
                weights_to_rows(0)
                bias(0)
                pe.wait_ge(sem("we_low"), 1)
                for g in range(G):
                    pe.wait_ge(sem("m1_low"), g + 1)
                    expert_pairs(g, 0)
                    if g + 1 < G:
                        pe.wait_ge(sem("m1_bias_added"), g + 1)
                        logits(g + 1)
                    expert_pairs(g, 1)
                    expert_pairs(g, 2)
                    if g + 1 < G:
                        weights_to_rows(g + 1)
                    expert_pairs(g, 3)
                    if g + 1 < G:
                        bias(g + 1)
                    if g + 2 < G:
                        pe.wait_ge(sem("m1_low"), g + 2)
                        transpose_rows("m1", g + 2)

            qkv(0)
            attention(0)
            project(0)
            ffn_weights()
            cross0()
            ffn()
            qkv(1)
            attention(1)
            project(1)
            cross1()
            experts()

        @block.vector
        def _(ve):
            v = nc.vector
            V = Steps(ve, sem("dve_step"))

            def group_stats(g, tag):
                V.sync()
                for t in range(GT):
                    ins = v.bn_stats(stats[:, t, :], x[:, GT * g + t, :])
                V(ins)
                V.sync()
                for t in range(GT):
                    ins = v.bn_aggr(mv[:, GT * g + t, :], stats[:, t, :])
                V(ins)
                V.sync()
                v.tensor_scalar(veps[:, GT * g:GT * g + GT], mv[:, GT * g:GT * g + GT, 1], LN_EPS, None, ALU.add)\
                    .then_inc(sem("var_ready"), 1)

            def normalise(g, tag):
                ve.wait_ge(sem("rstd_ready"), G * RSTD[tag] + g + 1)
                if g >= 2:
                    ve.wait_ge(sem("lnT"), G * TURN[tag] + g - 1)
                for t in range(GT):
                    tt = GT * g + t
                    ins = v.tensor_scalar(xn[:, g % 2, t, :], x[:, tt, :], mv[:, tt, 0:1], rstd[:, tt:tt + 1],
                                          ALU.subtract, ALU.mult)
                ins.then_inc(sem("xn_ready"), 1)

            V(v.memset(vext[:, :, D:D + H], 1.0))
            for g in range(G):
                ve.wait_ge(sem(f"x_loaded{g}"), 16)
                group_stats(g, "q0")

            ve.wait_ge(sem("w_qkv0"), 16 * 10)
            for k in range(K):
                v.tensor_tensor(wswap[:, k, :], wswap[:, k, :], sinr, ALU.mult)
                v.tensor_tensor(wqk[:, k, :], wqk[:, k, :], cosr, ALU.mult)
            v.tensor_tensor(bswap, bswap, sincol, ALU.mult)
            V(v.tensor_tensor(bqk[0][:, :], bqk[0][:, :], coscol, ALU.mult))
            V.sync()
            v.tensor_tensor(bqk[0][:, :], bqk[0][:, :], bswap, ALU.add)
            v.tensor_tensor(wqk[:, :, :], wqk[:, :, :], wswap, ALU.add).then_inc(sem("w_rotated"), 1)

            ve.wait_ge(sem("w_ctx"), 16 * 8)
            ve.wait_ge(sem("ctx_mm"), 1)
            for i in range(2 * B):
                ins = v.bn_stats(qstat[0:C, i, :], psum[0:C, i // 2, D * (i % 2):D * (i % 2) + D])
            V(ins)
            V.sync()
            for i in range(2 * B):
                ins = v.bn_aggr(qmv[0:C, i, :], qstat[0:C, i, :])
            V(ins)
            V.sync()
            v.tensor_scalar(qve[0:C, 0:4], qmv[0:C, 0:4, 1], X_EPS, None, ALU.add).then_inc(sem("ctx_var"), 1)
            ve.wait_ge(sem("ctx_rstd"), 1)
            for i in range(2 * B):
                ins = v.tensor_scalar(kvn[0:C, i // 2, D * (i % 2):D * (i % 2) + D], psum[0:C, i // 2, D * (i % 2):D * (i % 2) + D],
                                      qmv[0:C, i, 0:1], qrs[0:C, i:i + 1], ALU.subtract, ALU.mult)
            V(ins)
            for row, op in ((gB, ALU.mult), (bB, ALU.add)):
                V.sync()
                for i in range(2 * B):
                    part = kvn[0:C, i // 2, D * (i % 2):D * (i % 2) + D]
                    ins = v.tensor_tensor(part, part, row[0:C, :], op)
                V(ins)
            V.sync()
            for b in range(B):
                v.tensor_scalar(vext[0:C, b, 0:D], kvn[0:C, b, D:2 * D], mask[:, b:b + 1], None, ALU.mult)
                ins = v.tensor_scalar(kvn[0:C, b, 0:D], kvn[0:C, b, 0:D], 0.0, X_EPS, ALU.max, ALU.add)
            V(ins)
            V.sync()
            for b in range(B):
                ins = v.tensor_scalar(kvn[0:C, b, 0:D], kvn[0:C, b, 0:D], mask[:, b:b + 1], None, ALU.mult)
            ins.then_inc(sem("ctx_kv"), 1)
            ve.wait_ge(sem("kv_mm"), 1)
            for b in range(B):
                for m in range(K):
                    ins = v.tensor_tensor(kvbd[:, b, m, :], psum[:, 2 * b + m, 0:D + H], dmask[:, m, :], ALU.mult)
            ins.then_inc(sem("kvbd_ready"), 1)

            def qkv(layer):
                tag = f"q{layer}"
                v.memset(vs[:, :, :, HD:VW], 1.0).then_inc(sem("ones_ready"), 1)
                normalise(0, tag)
                if layer == 1:
                    ve.wait_ge(sem("w_qkv1"), 16 * 5)
                for g in range(G):
                    if g + 1 < G:
                        normalise(g + 1, tag)
                    b = g // 2
                    for n, u in qunits(g):
                        bank = 4 + n % 4
                        if u < 4:
                            ve.wait_ge(sem("high_ready"), 4 * G * layer + 4 * g + u + 1)
                            ins = v.scalar_tensor_tensor(out=hl[:, u % 2, 1, :], in0=psum[:, bank, :], scalar=bqk[layer][:, u:u + 1],
                                                         in1=hl[:, u % 2, 0, :].bitcast(F32), op0=ALU.add, op1=ALU.subtract)
                        else:
                            ve.wait_ge(sem("qkv_mm"), 6 * G * layer + n + 1)
                            for i in range(2):
                                kb = (GT * g + 2 * (u - 4) + i) % NK
                                ins = v.tensor_tensor(vall[:, b, :, kb, :], psum[:, bank, D * i:D * i + D].rearrange("p (h d) -> p h d", h=H),
                                                      bv.rearrange("p (h d) -> p h d", h=H), ALU.add)
                        ins.then_inc(sem("qkv_drained"), 1)

            def attention(layer):
                def take_max(head, par, qt):
                    ve.wait_ge(sem(f"max_scores{layer}"), NK * head + qt + 1)
                    v.tensor_reduce(nmax[:, par, qt:qt + 1], pflat[:, S * (qt % 2):S * (qt % 2) + a_cols(layer, qt)], AX, ALU.max,
                                    negate=True).then_inc(sem(f"max_taken{layer}"), 1)

                def split_max(head, par):
                    ve.wait_ge(sem(f"max_taken{layer}"), NK * (head + 1))
                    v.tensor_copy(tin[:, 0:NK].bitcast(F32R), nmax[:, par, :]).then_inc(sem("max_high"), 1)
                    ve.wait_ge(sem("max_high"), B * H * layer + head + 1)
                    v.tensor_tensor(tin[:, NK:2 * NK].bitcast(F32R), nmax[:, par, :], tin[:, 0:NK], ALU.subtract)\
                        .then_inc(sem("max_split"), 1)

                def max_to_rows(head, par):
                    ve.wait_ge(sem("max_turned"), B * H * layer + head + 1)
                    v.tensor_copy(trow[:, :], psum[0:2 * NK, 6 + par, 384:512]).then_inc(sem("max_rows"), 1)

                def heads(i, first):
                    for s in range(SLOTS):
                        head = SLOTS * i + s
                        for r in range(NK):
                            take_max(head, s % 2, r)
                            if r == 1 and not (first and s == 0):
                                max_to_rows(head - 1, (s + 1) % 2)
                        split_max(head, s % 2)

                heads(0, True)
                with ve.Fori(1, B * H // SLOTS) as i:
                    heads(i, False)
                max_to_rows(B * H - 1, 1)

            def project(layer, nxt):
                ve.wait_ge(sem(f"sums_loaded{layer}"), 16)
                for q in range(4):
                    rows = den[0:B * H, S // 4 * q:S // 4 * (q + 1)]
                    v.reciprocal(rows, rows).then_inc(sem("sums_inverted"), 1)
                for n in range(4 * B):
                    b, half, k = n // 4, n // 2 % 2, n % 2
                    ve.wait_ge(sem(f"attended_loaded{layer}_{b}"), 16 * K)
                    ve.wait_ge(sem("sums_spread"), 4 * B * layer + n + 1)
                    part = num[:, b, k, 512 * half:512 * half + 512]
                    v.tensor_tensor(part, part, psum[:, n % 4, :], ALU.mult).then_inc(sem("attn_ready"), 1)
                for u in range(2 * G):
                    ve.wait_ge(sem("proj_done"), 2 * G * layer + u + 1)
                    ve.wait_ge(sem("bias_added"), G * layer + u // 2 + 1)
                    ins = v.tensor_tensor(x[:, 2 * u:2 * u + 2, :], psum[:, 4 + u % 4, :].rearrange("p (t n) -> p t n", t=2),
                                          x[:, 2 * u:2 * u + 2, :], ALU.add)
                    ins.then_inc(sem("proj_drained"), 1)
                    if u % 2:
                        ve.wait_ge(sem("proj_drained"), 2 * G * layer + u + 1)
                        group_stats(u // 2, nxt)

            def ffn_weights():
                ve.wait_ge(sem("w_ffn"), 16)
                V(v.tensor_reduce(wsc, raw, AX, ALU.max, apply_absolute_value=True))
                V.sync()
                V(v.tensor_scalar(wsc, wsc, 1.0 / 7.0, TINY, ALU.mult, ALU.max))
                V.sync()
                V(v.reciprocal(wrc, wsc))
                V.sync()
                V(v.tensor_tensor(wint, raw, bc(wrc, QB, 2), ALU.mult))
                V.sync()
                v.tensor_tensor(raw, wint, bc(wsc, QB, 2), ALU.mult).then_inc(sem("w_dequant"), 1)

            def cross0(nxt):
                def query_stats(g):
                    ve.wait_ge(sem("x0_q"), g + 1)
                    row_stats(lambda t: psum[:, 2 + t // 2, D * (t % 2):D * (t % 2) + D], 0, "x0_var0")

                def row_stats(rows, lo, done):
                    for t in range(GT):
                        ins = v.bn_stats(qstat[:, t, :], rows(t))
                    V(ins)
                    V.sync()
                    for t in range(GT):
                        ins = v.bn_aggr(qmv[:, lo + t, :], qstat[:, t, :])
                    V(ins)
                    V.sync()
                    v.tensor_scalar(qve[:, lo:lo + GT], qmv[:, lo:lo + GT, 1], X_EPS, None, ALU.add).then_inc(sem(done), 1)

                def query_norm(g):
                    ve.wait_ge(sem("x0_rstd0"), g + 1)
                    if g >= 2:
                        ve.wait_ge(sem("x0_T2"), g - 1)
                    for t in range(GT):
                        ins = v.tensor_scalar(qn[:, g % 2, t, :], psum[:, 2 + t // 2, D * (t % 2):D * (t % 2) + D],
                                              qmv[:, t, 0:1], qrs[:, t:t + 1], ALU.subtract, ALU.mult)
                    ins.then_inc(sem("x0_qn"), 1)

                def output_rows(g):
                    ve.wait_ge(sem("x0_out"), g + 1)
                    for j in range(2):
                        ins = v.tensor_tensor(yb[:, 2 * j:2 * j + 2, :], psum[:, 6 + j, :].rearrange("p (t n) -> p t n", t=2),
                                              bc(bd[:, :], 2), ALU.add)
                    ins.then_inc(sem("x0_y"), 1)
                    ve.wait_ge(sem("x0_y"), g + 1)
                    row_stats(lambda t: yb[:, t, :], GT, "x0_var1")
                    ve.wait_ge(sem("x0_rstd1"), g + 1)
                    for t in range(GT):
                        ins = v.tensor_scalar(yb[:, t, :], yb[:, t, :], qmv[:, GT + t, 0:1], qrs[:, GT + t:GT + t + 1],
                                              ALU.subtract, ALU.mult)
                    V(ins)
                    V.sync()
                    V(v.tensor_tensor(yb, yb, bc(gB[:, :], GT), ALU.mult))
                    V.sync()
                    ve.wait_ge(sem("beta_added"), g + 1)
                    V(v.tensor_tensor(x[:, GT * g:GT * g + GT, :], yb, x[:, GT * g:GT * g + GT, :], ALU.add))
                    group_stats(g, nxt)

                normalise(0, "x0")
                query_stats(0)
                query_norm(0)
                for g in range(G):
                    if g + 1 < G:
                        normalise(g + 1, "x0")
                    ve.wait_ge(sem("x0_affine"), g + 1)
                    cols = qT[:, :, GN * (g % 2):GN * (g % 2) + GN]
                    v.tensor_scalar(cols, cols, 0.0, X_EPS, ALU.max, ALU.add).then_inc(sem("x0_qT"), 1)
                    if g + 1 < G:
                        query_stats(g + 1)
                        query_norm(g + 1)
                    if g % 2 == 0:
                        continue
                    for half in range(2):
                        ve.wait_ge(sem("x0_kv"), 2 * (g // 2) + half + 1)
                        V(v.tensor_scalar(zden, psum[:, 4, 0:NK * NK], X_EPS, None, ALU.add))
                        V.sync()
                        V(v.reciprocal(zden, zden))
                        V.sync()
                        for i in range(0, NK, 4):
                            lo = HD * (NK * half + i)
                            for n in range(4):
                                ins = v.tensor_tensor(att[:, :, lo + HD * n:lo + HD * n + HD],
                                                      psum[:, 6 + i // 4, P * n:P * n + P].rearrange("p (t e) -> p t e", e=HD),
                                                      bc(zden[:, NK * (i + n):NK * (i + n) + NK], HD, 2), ALU.mult)
                        ins.then_inc(sem("x0_att"), 1)
                    for gg in (g - 1, g):
                        output_rows(gg)

            def global_scale(n, maxima, cols, c):
                V.sync()
                v.tensor_reduce(sc[:, 0:1], maxima, AX, ALU.max).then_inc(sem("gm_col"), 1)
                ve.wait_ge(sem("gm_row"), n + 1)
                v.tensor_reduce(sc[0:1, 1:2], psum[0:1, 7, 0:P], AX, ALU.max).then_inc(sem("gm_one"), 1)
                ve.wait_ge(sem("gm_all"), n + 1)
                s_col, inv = sc[:, cols:cols + 1], sc[:, cols + 1:cols + 2]
                V(v.tensor_scalar(s_col, psum[:, 7, 256:257], c, 1.0 / QMAX, ALU.mult, ALU.mult))
                V.sync()
                V(v.tensor_scalar(s_col, s_col, TINY, None, ALU.max))
                V.sync()
                V(v.reciprocal(inv, s_col))
                V.sync()
                V(v.tensor_scalar(inv, inv, c, None, ALU.mult))
                V.sync()

            MAGIC = 12582912.0

            def ffn(nxt):
                SX, SU, SG, SP, SO, CP, CR = 10, 15, 20, 25, 30, 35, 36
                for g in range(G):
                    ve.wait_ge(sem("rstd_ready"), G * RSTD["f0"] + g + 1)
                    for t in range(GT * g, GT * g + GT):
                        ins = v.tensor_scalar(xq[:, t, :], x[:, t, :], mv[:, t, 0:1], rstd[:, t:t + 1], ALU.subtract, ALU.mult)
                    V(ins)
                    V.sync()
                    V(v.tensor_reduce(am[:, g:g + 1], at(12288 + 1024 * g, 1024), AX, ALU.max, apply_absolute_value=True))
                global_scale(0, am[:, 0:G], SX, 1.0)
                for g in range(G):
                    rows = at(12288 + 1024 * g, 1024)
                    V(v.tensor_scalar(rows, rows, sc[:, SX + 1:SX + 2], MAGIC, ALU.mult, ALU.add))
                    V.sync()
                    v.tensor_scalar(rows, rows, -MAGIC, None, ALU.add).then_inc(sem("xq_ready"), 1)

                def product_max(m, a, b):
                    V(v.tensor_tensor(act[:, m, :], a, b, ALU.mult))
                    V.sync()
                    V(v.tensor_reduce(am[:, m:m + 1], act[:, m, :], AX, ALU.max, apply_absolute_value=True))

                def unit_maxima(first):
                    for n in range(first, first + FM * G):
                        m, g = divmod(n % (FM * G), G)
                        ve.wait_ge(sem("f_evac"), n + 1)
                        ins = v.tensor_reduce(am[:, n:n + 1], act[:, m, GN * g:GN * g + GN], AX, ALU.max, apply_absolute_value=True)
                    V(ins)

                unit_maxima(0)
                global_scale(1, am[:, 0:FM * G], SU, sc[:, SX:SX + 1])
                for m in range(FM):
                    v.tensor_scalar(qup[:, m, :], act[:, m, :], sc[:, SU + 1:SU + 2], None, ALU.mult).then_inc(sem("qup_ready"), 1)
                unit_maxima(FM * G)
                global_scale(2, am[:, FM * G:2 * FM * G], SG, sc[:, SX:SX + 1])
                for m in range(FM):
                    v.tensor_scalar(qgate[:, m, :], act[:, m, :], sc[:, SG + 1:SG + 2], None, ALU.mult).then_inc(sem("qgate_ready"), 1)
                V(v.tensor_scalar(sc[:, CP:CP + 1], sc[:, SG:SG + 1], 1.0 / 65536.0, None, ALU.mult))
                for m in range(FM):
                    ve.wait_ge(sem("sigmoid_ready"), m + 1)
                    V(v.tensor_scalar(zint[:, m % 4, :], act[:, m, :], 65536.0, 65535.0, ALU.mult, ALU.min))
                    V.sync()
                    product_max(m, zint[:, m % 4, :], qgate[:, m, :])
                global_scale(3, am[:, 0:FM], SP, sc[:, CP:CP + 1])
                v.tensor_scalar(sc[:, CR:CR + 1], sc[:, SP:SP + 1], sc[:, SU:SU + 1], None, ALU.mult).then_inc(sem("p_scaled"), 1)
                for m in range(FM):
                    ve.wait_ge(sem("qp_ready"), m + 1)
                    product_max(m, qgate[:, m, :], qup[:, m, :])
                global_scale(4, am[:, 0:FM], SO, sc[:, CR:CR + 1])
                for g in range(G):
                    cols = act[:, :, GN * g:GN * g + GN]
                    V(v.tensor_scalar(cols, cols, sc[:, SO + 1:SO + 2], MAGIC, ALU.mult, ALU.add))
                    V.sync()
                    v.tensor_scalar(cols, cols, -MAGIC, None, ALU.add).then_inc(sem("q3_ready"), 1)
                for u in range(2 * G):
                    ve.wait_ge(sem("down_mm"), u + 1)
                    v.scalar_tensor_tensor(out=x[:, 2 * u:2 * u + 2, :], in0=psum[:, u % 4, :].rearrange("p (t n) -> p t n", t=2),
                                           scalar=sc[:, SO:SO + 1], in1=x[:, 2 * u:2 * u + 2, :],
                                           op0=ALU.mult, op1=ALU.add).then_inc(sem("down_drained"), 1)
                    if u % 2:
                        ve.wait_ge(sem("down_drained"), u + 1)
                        group_stats(u // 2, nxt)

            def cross1(nxt):
                normalise(0, "x1")
                for g in range(G):
                    if g + 1 < G:
                        normalise(g + 1, "x1")
                    ve.wait_ge(sem("x1_scores"), g + 1)
                    V(v.tensor_reduce(qve[:, GT:2 * GT], psum[:, 2, 0:GT * C].rearrange("p (t c) -> p t c", t=GT), AX, ALU.max, negate=True))
                    V.sync()
                    v.tensor_scalar(qve[:, 0:GT], qve[:, GT:2 * GT], D ** -0.5, None, ALU.mult).then_inc(sem("x1_max"), 1)
                    ve.wait_ge(sem("x1_exp"), g + 1)
                    V(v.reciprocal(qrs[:, GT:2 * GT], qrs[:, 0:GT]))
                    V.sync()
                    ve.wait_ge(sem("x1_out"), g + 1)
                    for t in range(GT):
                        tt = GT * g + t
                        ins = v.scalar_tensor_tensor(out=x[:, tt, :], in0=psum[:, 6 + t // 2, D * (t % 2):D * (t % 2) + D],
                                                     scalar=qrs[:, GT + t:GT + t + 1], in1=x[:, tt, :], op0=ALU.mult, op1=ALU.add)
                    ins.then_inc(sem("x1_added"), 1)
                    ve.wait_ge(sem("x1_added"), g + 1)
                    group_stats(g, nxt)

            def experts():
                def low_parts(g):
                    ve.wait_ge(sem("xT_ready"), G * TURN["m1"] + g + 1)
                    if g >= 2:
                        ve.wait_ge(sem("m1_mm"), 16 * (g - 1))
                    for k in range(K):
                        ins = v.tensor_tensor(xhl[:, g % 2, 1, k, :], psum[:, k, :], xhl[:, g % 2, 0, k, :].bitcast(F32), ALU.subtract)
                    ins.then_inc(sem("m1_low"), 1)

                def routing(g):
                    ve.wait_ge(sem("m1_logits"), g + 1)
                    V(v.tensor_tensor(lg, psum[:, 2, 0:GT * E].rearrange("p (t e) -> p t e", t=GT), bc(rb[:, :], GT), ALU.add))
                    V.sync()
                    V(v.tensor_reduce(lm, lg, AX, ALU.max))
                    V.sync()
                    V(v.tensor_tensor(ex, lg, bc(lm, E, 2), ALU.subtract))
                    V.sync()
                    V(v.tensor_scalar(best[:, g % 2], ex, 0.0, None, ALU.is_equal))
                    V.sync()
                    v.tensor_tensor(mw, best[:, g % 2], bc(rank[:, :], GT), ALU.mult).then_inc(sem("m1_shift"), 1)
                    ve.wait_ge(sem("m1_shift"), g + 1)
                    V(v.tensor_reduce(lm, mw, AX, ALU.max))
                    V.sync()
                    V(v.tensor_tensor(best[:, g % 2], mw, bc(lm, E, 2), ALU.is_equal))
                    ve.wait_ge(sem("m1_exp"), g + 1)
                    V.sync()
                    V(v.tensor_reduce(lm, ex, AX, ALU.add))
                    V.sync()
                    V(v.reciprocal(lm, lm))
                    V.sync()
                    v.tensor_tensor(mw, best[:, g % 2], bc(lm, E, 2), ALU.mult).then_inc(sem("m1_mw"), 1)
                    ve.wait_ge(sem("m1_mw"), g + 1)
                    V(v.tensor_copy(best[:, g % 2], mw))
                    V.sync()

                def add_bias(g):
                    ve.wait_ge(sem("m1_bias"), g + 1)
                    for j in range(2):
                        t0 = GT * g + 2 * j
                        ins = v.tensor_tensor(x[:, t0:t0 + 2, :], psum[:, 2 + j, :].rearrange("p (t n) -> p t n", t=2),
                                              x[:, t0:t0 + 2, :], ALU.add)
                    V(ins)
                    V.sync()
                    ve.sem_inc(sem("m1_bias_added"), 1)

                def add_experts(g, t):
                    for c in range(E // 2):
                        n = 16 * g + 4 * t + c
                        ve.wait_ge(sem("m1_mm"), n + 1)
                        for e in (2 * c, 2 * c + 1):
                            ins = v.scalar_tensor_tensor(out=x[:, GT * g + t, :], in0=psum[:, 4 + n % 4, D * (e % 2):D * (e % 2) + D],
                                                         scalar=best[:, g % 2, t, e:e + 1], in1=x[:, GT * g + t, :], op0=ALU.mult, op1=ALU.add)
                            if e % 2 == 0:
                                V(ins)
                                V.sync()
                        ins.then_inc(sem("m1_added"), 1)
                        ve.wait_ge(sem("m1_added"), n + 1)

                normalise(0, "m1")
                low_parts(0)
                normalise(1, "m1")
                routing(0)
                low_parts(1)
                add_bias(0)
                for g in range(G):
                    add_experts(g, 0)
                    if g + 1 < G:
                        routing(g + 1)
                    add_experts(g, 1)
                    if g + 2 < G:
                        normalise(g + 2, "m1")
                    add_experts(g, 2)
                    add_experts(g, 3)
                    if g + 1 < G:
                        add_bias(g + 1)
                    if g + 2 < G:
                        low_parts(g + 2)
                    ve.sem_inc(sem("moe_done"), 1)

            qkv(0)
            attention(0)
            project(0, "x0")
            ffn_weights()
            cross0("f0")
            ffn("q1")
            qkv(1)
            attention(1)
            project(1, "x1")
            cross1("m1")
            experts()


def rope_tables():
    inv = (1.0 / 10000.0 ** (np.arange(0, HD, 2, dtype=np.float32) / HD)).astype(np.float32)
    f = np.arange(H, dtype=np.float32)[:, None] * inv[None, :]
    cos, sin = np.cos(f), np.sin(f)
    c = np.concatenate([cos, cos], axis=1).reshape(-1)
    s = np.concatenate([-sin, sin], axis=1).reshape(-1)
    return np.tile(c, 2), np.tile(s, 2)


def kernel(x, ctx_1024, mask_BxS2_ff1, L0_attn_qkv_w, L0_attn_qkv_b, L0_attn_out_w, L0_attn_out_b,
           L0_xattn_wq, L0_xattn_wk, L0_xattn_wv, L0_xattn_ln_gamma, L0_xattn_ln_beta, L0_xattn_dense_w,
           L0_xattn_dense_b, L0_ffn_w_gate, L0_ffn_w_up, L0_ffn_w_down, L1_attn_W_attn, L1_attn_b_attn,
           L1_attn_W_proj, L1_attn_b_proj, L1_xattn_Wq, L1_xattn_Wkv, L1_ffn_router_w, L1_ffn_router_b,
           L1_ffn_expert_w, L1_ffn_expert_b):
    import concourse.bacc as bacc
    from concourse.bass_utils import run_bass_kernel_spmd

    def halves(w):
        w = np.asarray(w)
        return w.reshape(-1, P, w.shape[-1]).transpose(1, 0, 2)

    def columns(v):
        return np.asarray(v).reshape(-1, P).T

    def split_qkv(w):
        w = np.asarray(w)
        w = w.reshape(w.shape[:-1] + (H, 3, HD))
        return w[..., 0, :].reshape(w.shape[:-3] + (D,)), w[..., 1, :].reshape(w.shape[:-3] + (D,)), w[..., 2, :].reshape(w.shape[:-3] + (D,))

    def swap(w):
        r = w.reshape(w.shape[:-1] + (-1, 2, HD // 2))
        return r[..., ::-1, :].reshape(w.shape)

    arrays = {}
    arrays["x"] = np.asarray(x).reshape(T, P, D).transpose(1, 0, 2)
    for i, (w, bias, wo, bo) in enumerate(((L0_attn_qkv_w, L0_attn_qkv_b, L0_attn_out_w, L0_attn_out_b),
                                           (L1_attn_W_attn, L1_attn_b_attn, L1_attn_W_proj, L1_attn_b_proj))):
        q, k, vv = split_qkv(w)
        qk = np.concatenate([q, k], axis=1)
        qb, kb, vb = split_qkv(bias)
        bqk = np.concatenate([qb, kb])
        arrays[f"wqk{i}"], arrays[f"wv{i}"], arrays[f"bqk{i}"], arrays[f"bv{i}"] = halves(qk), halves(vv), columns(bqk), vb
        arrays[f"wo{i}"], arrays[f"bo{i}"] = halves(wo), np.asarray(bo)
        if i == 0:
            arrays["wqks"], arrays["bqks"] = halves(swap(qk)), columns(swap(bqk))
    cos, sin = rope_tables()
    arrays["cos"], arrays["sin"] = np.tile(cos, (P, 1)), np.tile(sin, (P, 1))
    arrays["coscol"], arrays["sincol"] = columns(cos), columns(sin)
    arrays["ctxT"] = halves(np.asarray(ctx_1024).reshape(B * C, D).T)
    arrays["mask"] = np.asarray(mask_BxS2_ff1).T
    arrays["xwq"] = halves(L0_xattn_wq)
    arrays["xwkv"] = halves(np.concatenate([np.asarray(L0_xattn_wk), np.asarray(L0_xattn_wv)], axis=1))
    arrays["xwd"] = halves(L0_xattn_dense_w)
    arrays["g"], arrays["b"], arrays["bd"] = (np.asarray(a) for a in (L0_xattn_ln_gamma, L0_xattn_ln_beta, L0_xattn_dense_b))
    arrays["gcol"], arrays["bcol"] = columns(L0_xattn_ln_gamma), columns(L0_xattn_ln_beta)
    head = np.arange(D) // HD
    same = np.concatenate([head[:, None] == head[None, :], head[:, None] == np.arange(H)[None, :]], axis=1)
    pick = np.zeros((B * H, B, D), np.float32)
    for b in range(B):
        pick[b * H + head, b, np.arange(D)] = 1.0
    arrays["pick"] = pick
    arrays["dmask"] = halves(same.astype(np.float32))
    arrays["w1q"] = halves(np.asarray(L1_xattn_Wq).T)
    arrays["w1kv"] = halves(L1_xattn_Wkv)
    flat = lambda w: halves(w).reshape(P, -1)
    arrays["ffw"] = np.concatenate([flat(L0_ffn_w_gate), flat(L0_ffn_w_up), flat(L0_ffn_w_down)], axis=1)
    arrays["rw"] = halves(np.asarray(L1_ffn_router_w).T)
    arrays["rb"], arrays["eb"] = np.asarray(L1_ffn_router_b), np.asarray(L1_ffn_expert_b)
    arrays["we"] = halves(np.asarray(L1_ffn_expert_w).transpose(2, 0, 1).reshape(D, E * D))
    arrays["rank"] = np.tile(np.arange(E, 0, -1, dtype=np.float32), (P, 1))
    arrays["ident"] = np.eye(P, dtype=np.float32)
    arrays["identb"] = np.eye(P, dtype=mybir.dt.np(BF16))
    above = np.triu(np.full((P, P), NEG, np.float32), 1)
    arrays["causal"] = np.stack([above, above.T], axis=1).astype(mybir.dt.np(BF16))

    nc = bacc.Bacc("TRN2", target_bir_lowering=False, num_devices=1)
    dram, given = {}, {}
    for name, a in arrays.items():
        given[f"in_{name}"] = np.ascontiguousarray(a)
        dram[name] = nc.dram_tensor(f"in_{name}", a.shape, mybir.dt.from_np(a.dtype), kind="ExternalInput").ap()
    out = nc.dram_tensor("out", (P, T, D), F32, kind="ExternalOutput").ap()
    build(nc, dram, out)
    r = run_bass_kernel_spmd(nc, [given], core_ids=[0])
    return np.asarray(r.results[0]["out"]).transpose(1, 0, 2).reshape(B, S, D)
```

```python
from contextlib import ExitStack

import numpy as np

import concourse.bass as bass
from concourse import mybir

F32 = mybir.dt.float32
F32R = mybir.dt.float32r
BF16 = mybir.dt.bfloat16
I16 = mybir.dt.int16
U16 = mybir.dt.uint16
ALU = mybir.AluOpType
ACT = mybir.ActivationFunctionType
AX = mybir.AxisListType.X

P = 128
B, S, D = 2, 1024, 256
H, HD = 16, 16
T = B * S // P
GT = 4
G = T // GT
GN = GT * P
K = D // P
C = 77
FF = 768
FM = FF // P
QB = 32
E = 8
NK = S // P
HPF = P // HD
PARTS = 4
PROD = PARTS * HD
STK = 96
STKM = 128
SLOTS = 4
VW = 2 * HD
LEAD = 15
RSTD = {"q0": 0, "x0": 1, "f0": 2, "q1": 3, "x1": 4, "m1": 5}
TURN = {"q0": 0, "x0": 1, "q1": 2, "x1": 3, "m1": 4}
NEG = -1e30
W_REST = 15
LN_EPS = 1e-5
X_EPS = 1e-6
QMAX = 32767.0
TINY = 1e-12


class Steps:

    def __init__(self, eng, sem):
        self.eng, self.sem, self.n = eng, sem, 0

    def __call__(self, ins):
        self.n += 1
        ins.then_inc(self.sem, 1)

    def sync(self):
        self.eng.wait_ge(self.sem, self.n)


def build(nc, d, out):
    ctx = ExitStack()
    with ctx:
        def sb(name, shape, dt=F32):
            return ctx.enter_context(nc.sbuf_tensor(name, shape, dt))

        made = {}

        def sem(name):
            if name not in made:
                made[name] = ctx.enter_context(nc.semaphore(name))
            return made[name]

        x = sb("x", [P, T, D])
        xx = sb("xx", [P, 2 * K * GN * 2])
        xn = xx[:, 0:2 * GT * D].rearrange("p (s t n) -> p s t n", s=2, t=GT)
        xT = xx[:, 2 * GT * D:].rearrange("p (s k n) -> p s k n", s=2, k=K)
        xqT = xx[:, :].rearrange("p (k n) -> p k n", k=K)
        ident = sb("ident", [P, P])
        identb = sb("identb", [P, P], BF16)
        causal = sb("causal", [P, 2, P], BF16)
        stats = sb("stats", [P, GT, 6])
        mv = sb("mv", [P, T, 2])
        veps = sb("veps", [P, T])
        rstd = sb("rstd", [P, T])
        mhalf = sb("mhalf", [P, T])
        ones = sb("ones", [P, P])
        bqk = [sb(f"bqk{i}", [P, 2 * K]) for i in range(2)]
        mask = sb("mask", [C, B])
        gcol = sb("gcol", [P, K])
        bcol = sb("bcol", [P, K])
        rw = sb("rw", [P, K, E])
        rb = sb("rb", [P, E])
        rank = sb("rank", [P, E])
        eb = sb("eb", [E, D])
        km = sb("km", [P, B, K, C])
        v1 = sb("v1", [C, B, D])
        picked = sb("picked", [2 * B * H, B, D])
        pick = sb("pick", [2 * B * H, B, D], F32R)
        qstat = sb("qstat", [P, GT, 6])
        qmv = sb("qmv", [P, 2 * GT, 2])
        qve = sb("qve", [P, 2 * GT])
        qrs = sb("qrs", [P, 2 * GT])
        tin = sb("tin", [P, 2 * NK])
        trow = sb("trow", [2 * NK, P])
        nmax = sb("nmax", [P, 2, NK])
        qs = sb("qs", [P, SLOTS, S], F32R)
        ks = sb("ks", [P, SLOTS, S], F32R)
        xhl = sb("xhl", [P, 2, 2, K, GN], F32R)
        hl = xhl[:, 0, :, :, :]
        am = sb("am", [P, 4 * G * FM])
        sc = sb("sc", [P, 40])

        BIG, WTS = 24576, 4608
        arena = sb("arena", [P, BIG + WTS])

        def at(off, n, *shape, dt=F32):
            v = arena[:, off:off + n]
            if dt != F32:
                v = v.bitcast(dt)
            names = "abcde"[:len(shape)]
            if len(shape) > 1:
                v = v.rearrange(f"p ({' '.join(names)}) -> p {' '.join(names)}", **dict(zip(names[:-1], shape)))
            return v

        vall = at(0, 4096, B, H, NK, HD)
        probs = at(4096, 4096, 4, S)
        osb = at(8192, 1024, SLOTS, 2 * P)
        vs = at(9216, SLOTS * NK * VW, SLOTS, NK, VW)
        num = at(0, 4096, B, K, S)
        den = at(4096, 1024, S)
        wqk = at(BIG, 1024, K, 2 * D)
        wv = at(BIG + 1024, 512, K, D)
        wo = at(23488, 512, K, D)
        bv = at(BIG + 2048, 256, D)
        bo = at(24000, 256, D)
        wswap = at(12288, 1024, K, 2 * D)
        cosr = at(13312, 512, 2 * D)
        sinr = at(13824, 512, 2 * D)
        bswap = at(14336, 4, 4)
        coscol = at(14340, 4, 4)
        sincol = at(14344, 4, 4)
        ctxT = at(14352, K * B * C, K, B * C)
        xwkv = at(14720, 1024, K, 2 * D)
        w1q = at(15744, 512, K, D)
        w1kv = at(16256, 1024, K, 2 * D)
        dmask = at(17280, K * (D + H), K, D + H)
        kvn = at(17824, 1024, B, 2 * D)
        vext = at(18848, B * (D + H), B, D + H)
        k1T = at(19392, K * B * C, K, B * C)
        xwq = at(20608, 512, K, D)
        xwd = at(21120, 512, K, D)
        gB = at(21632, 256, D)
        bB = at(21888, 256, D)
        bd = at(22144, 256, D)
        KV = 4 * HD + 4
        kvbd = at(22400, B * K * 2 * KV, B, K, 2, KV)
        qn = at(12288, 2048, 2, GT, D)
        qT = at(14336, 2048, K, S)
        att = at(16384, 2048, NK, D)
        attT = at(18432, 1024, K, GN)
        yb = at(19456, 1024, GT, D)
        zden = at(20480, 2 * NK * NK, 2, NK * NK)
        pm = at(12288, GT * C + 4, GT * C + 4)
        pT = at(12672, GN, GN)
        we = at(17408, K * E * D, K, E * D)
        wehl = [st[:, :, :].rearrange("p s n -> p (s n)").rearrange("p (k n) -> p k n", k=K) for st in (qs, ks)]
        x32 = at(13312, 2 * K * GN, 2, K, GN)
        best = at(12960, 2 * GT * E, 2, GT, E)
        RAW = 12288
        raw = at(RAW, WTS, 144, QB)
        rawg = at(RAW, FM * D, FM, D)
        rawu = at(RAW + FM * D, FM * D, FM, D)
        rawd = at(RAW + 2 * FM * D, K * FF, K, FF)
        wint = at(BIG + WTS // 2, WTS // 2, 144, QB, dt=I16)
        wsc = at(19392, 144, 144)
        wrc = at(19392 + 144, 144, 144)
        wgp = qs[:, :, :].rearrange("p s n -> p (s n)")[:, S:S + 2 * K * FF]
        wup = ks[:, :, :].rearrange("p s n -> p (s n)")[:, 0:2 * K * FF]
        wgT, wuT = (w.rearrange("p (x k n) -> p x k n", x=2, k=K) for w in (wgp, wup))
        wdT = at(BIG + WTS // 2, FM * D, FM, D)
        act = at(0, FM * T * P, FM, T * P)
        qup = at(12288, FM * T * P // 2, FM, T * P, dt=I16)
        qgate = at(12288 + 6144, FM * T * P // 2, FM, T * P, dt=I16)
        xq = at(0, T * D, T, D)
        zint = xx[:, :].bitcast(U16).rearrange("p (s n) -> p s n", s=4)

        psum = ctx.enter_context(nc.psum_tensor("psum", [P, 8, 512], F32))
        pflat = psum[:, :, :].rearrange("p b n -> p (b n)")

        lg = at(12288, GT * E, GT, E)
        ex = at(12320, GT * E, GT, E)
        mw = at(12352, GT * E, GT, E)
        lm = at(12384, GT, GT)
        mwT = at(12416, GN, GN)

        qd = nc.dram_tensor("qd", (B * H, 3 * HD, S), F32).ap()
        kd = nc.dram_tensor("kd", (B * H, 2 * HD, S), F32).ap()
        od = nc.dram_tensor("od", (B * H, HD + 1, S), F32).ap()

        def kv_place(half, i):
            return ((6, 7, 4), (5, 0, 1))[half][i // 3], 2 * KV * (i % 3)

        block = ctx.enter_context(nc.Block())

        def qunits(g):
            return [(6 * g + u, u) for u in range(6)]

        def a_cols(layer, qt):
            return S if layer == 0 else P * (qt + 1)

        def b_units(layer, kb):
            lo = 0 if layer == 0 else P * kb
            return [(max(lo, a), a + 512) for a in (0, 512) if lo < a + 512]

        def b_before(layer, kb):
            return sum(len(b_units(layer, i)) for i in range(kb))

        def pv_blocks(layer, kb, j):
            return [q for q in (j, NK - 1 - j) if layer == 0 or q >= kb]

        @block.sync
        def _(sp):
            def load(dst, src, name):
                sp.dma_start(dst, src).then_inc(sem(name), 16)

            def load_x(g):
                load(x[:, GT * g:GT * g + GT, :], d["x"][:, GT * g:GT * g + GT, :], f"x_loaded{g}")

            load_x(0)
            load(ident[:, :], d["ident"], "const_loaded")
            load(wqk, d["wqk0"], "w_qkv0")
            load(wswap, d["wqks"], "w_qkv0")
            load(cosr, d["cos"], "w_qkv0")
            load(sinr, d["sin"], "w_qkv0")
            load(bqk[0][:, :], d["bqk0"], "w_qkv0")
            load(bswap, d["bqks"], "w_qkv0")
            load(coscol, d["coscol"], "w_qkv0")
            load(sincol, d["sincol"], "w_qkv0")
            load(wv, d["wv0"], "w_qkv0")
            load(bv, d["bv0"].partition_broadcast(P), "w_qkv0")
            for g in range(1, G):
                load_x(g)
            load(wo, d["wo0"], "w_rest")
            load(bo, d["bo0"].partition_broadcast(P), "w_rest")
            load(xwq[:, :, :], d["xwq"], "w_rest")
            load(xwd[:, :, :], d["xwd"], "w_rest")
            load(bd[:, :], d["bd"].partition_broadcast(P), "w_rest")
            load(gcol[:, :], d["gcol"], "w_rest")
            load(bcol[:, :], d["bcol"], "w_rest")
            load(bqk[1][:, :], d["bqk1"], "w_rest")
            load(rw[:, :, :], d["rw"], "w_rest")
            load(rb[:, :], d["rb"].partition_broadcast(P), "w_rest")
            load(eb[:, :], d["eb"], "w_rest")
            load(rank[:, :], d["rank"], "w_rest")
            load(causal[:, :, :], d["causal"], "w_rest")
            load(picked[:, :, :], d["pick"], "w_rest")
            load(identb[:, :], d["identb"], "w_rest")

            def load_stack(layer, s, bh):
                loaded = sem(f"stack_loaded{layer}_{s}")
                sp.dma_start(qs[0:2 * HD, s, :].bitcast(F32), qd[bh, 0:2 * HD, :]).then_inc(loaded, 16)
                sp.dma_start(qs[2 * HD:4 * HD, s, :].bitcast(F32), qd[bh, HD:3 * HD, :]).then_inc(loaded, 16)
                sp.dma_start(ks[0:2 * HD, s, :].bitcast(F32), kd[bh, :, :]).then_inc(loaded, 16)
                sp.dma_start(ks[2 * HD:4 * HD, s, :].bitcast(F32), kd[bh, :, :]).then_inc(loaded, 16)

            def store_split(layer):
                for g in range(G):
                    if layer == 0 and g == 1:
                        sp.wait_ge(sem("w_rotated"), 1)
                        sp.wait_ge(sem("km_mm"), 1)
                        load(at(RAW, WTS), d["ffw"], "w_ffn")
                    if g == G // B:
                        for u in range(4):
                            sp.wait_ge(sem(f"split_stored{layer}_{u}"), 16 * g * (3 if u < K else 2))
                    b, c0 = divmod(g * GN, S)
                    for n, u in qunits(g)[:4]:
                        is_q, ft = u < K, u % K
                        sp.wait_ge(sem("qkv_drained"), 6 * G * layer + n + 1)
                        h0 = b * H + ft * HPF
                        for part, src in enumerate((0, 1, 0) if is_q else (0, 1)):
                            dst = (qd if is_q else kd)[h0:h0 + HPF, HD * part:HD * part + HD, c0:c0 + GN]
                            sp.dma_start(dst, hl[:, u % 2, src, :].bitcast(F32)).then_inc(sem(f"split_stored{layer}_{u}"), 16)
                    if g >= G // B:
                        load_stack(layer, g - G // B, g - G // B)
                for st in range(G - G // B, SLOTS):
                    load_stack(layer, st, st)
                for u in range(4):
                    sp.wait_ge(sem(f"split_stored{layer}_{u}"), 16 * G * (3 if u < K else 2))

            def attention(layer):
                def load_max(s, head):
                    sp.wait_ge(sem("max_rows"), B * H * layer + head + 1)
                    for part in range(2):
                        sp.dma_start(qs[STK + part:STK + part + 1, s, :].bitcast(F32).rearrange("p (t c) -> p t c", t=NK),
                                     trow[NK * part:NK * part + NK, :]).then_inc(sem(f"max_loaded{layer}_{s}"), 16)

                load_max(0, 0)

                def heads(i, last):
                    for s in range(SLOTS):
                        head = SLOTS * i + s
                        if not (last and s == SLOTS - 1):
                            load_max((s + 1) % SLOTS, head + 1)
                        if not last:
                            sp.wait_ge(sem(f"scores{layer}"), b_before(layer, NK) * (head + 1))
                            load_stack(layer, s, head + SLOTS)

                with sp.Fori(0, B * H // SLOTS - 1) as i:
                    heads(i, False)
                heads(B * H // SLOTS - 1, True)

            def load_attended(layer):
                for s in range(SLOTS):
                    sp.wait_ge(sem(f"out_stored{layer}_{s}"), 64 * (B * H // SLOTS))
                load(den[0:B * H, :], od[:, HD, :], f"sums_loaded{layer}")
                for b in range(B):
                    for k in range(K):
                        h0 = b * H + k * HPF
                        load(num[:, b, k, :], od[h0:h0 + HPF, 0:HD, :], f"attended_loaded{layer}_{b}")

            store_split(0)
            attention(0)
            load_attended(0)
            load(wqk, d["wqk1"], "w_qkv1")
            load(wv, d["wv1"], "w_qkv1")
            load(bv, d["bv1"].partition_broadcast(P), "w_qkv1")
            sp.wait_ge(sem("down_mm"), 2 * G)
            load(wo, d["wo1"], "w_out1")
            load(bo, d["bo1"].partition_broadcast(P), "w_out1")
            store_split(1)
            attention(1)
            load_attended(1)
            load(we, d["we"], "w_experts")
            for g in range(G):
                sp.wait_ge(sem("moe_done"), g + 1)
                sp.dma_start(out[:, GT * g:GT * g + GT, :], x[:, GT * g:GT * g + GT, :]).then_inc(sem("out_stored"), 16)
            sp.wait_ge(sem("out_stored"), 16 * G)

        def bc(ap, n, axis=1):
            shape = list(ap.shape)
            shape.insert(axis, n)
            return ap.unsqueeze(axis).broadcast_to(shape)

        @block.gpsimd
        def _(gp):
            gp.memset(mhalf[:, :], -0.5).then_inc(sem("pool_const"), 1)
            gp.memset(ones[:, :], 1.0).then_inc(sem("pool_const"), 1)
            gp.wait_ge(sem("pool_const"), 2)

            def power(dst, src, need, n, done):
                gp.wait_ge(sem(need), n)
                gp.tensor_tensor(dst, src, mhalf[0:dst.shape[0], 0:dst.shape[1]], ALU.pow).then_inc(sem(done), 1)

            def rstd_groups(tag, g):
                power(rstd[:, GT * g:GT * g + GT], veps[:, GT * g:GT * g + GT], "var_ready", G * RSTD[tag] + g + 1, "rstd_ready")

            def add_rows(g, row, done):
                for t in range(GT * g, GT * g + GT):
                    ins = gp.tensor_tensor(x[:, t, :], x[:, t, :], row, ALU.add)
                ins.then_inc(sem(done), 1)

            def attention(layer):
                vheads = at(0, 4096, B * H, NK, HD)

                def copy_values(s, bh):
                    gp.tensor_copy(vs[:, s, :, 0:HD], vheads[:, bh, :, :]).then_inc(sem("values_copied"), 1)

                def store_out(s, head):
                    gp.wait_ge(sem(f"out_ready{layer}"), head + 3)
                    for j in range(4):
                        dst = od[head, :, :].rearrange("r (q c) -> r q c", q=NK)[:, j:NK - j:NK - 1 - 2 * j, :]
                        src = osb[32 * j:32 * j + HD + 1, s, :].rearrange("r (q c) -> r q c", q=2)
                        gp.dma_start(dst, src).then_inc(sem(f"out_stored{layer}_{s}"), 16)

                gp.wait_ge(sem("qkv_drained"), 6 * G * layer + 6 * G)
                for s in range(SLOTS):
                    copy_values(s, s)
                gp.wait_ge(sem("w_rest" if layer == 0 else "w_out1"), 16 * (W_REST if layer == 0 else 2))
                for g in range(G):
                    add_rows(g, bo, "bias_added")
                with gp.Fori(0, B * H // SLOTS - 1) as i:
                    for s in range(SLOTS):
                        store_out(s, SLOTS * i + s)
                        copy_values(s, SLOTS * i + s + SLOTS)
                for s in range(SLOTS):
                    store_out(s, B * H - SLOTS + s)

            def stack_rows(layer):
                for n, stack in enumerate((qs, ks)):
                    gp.memset(stack[PROD:STKM, :, :].bitcast(F32), 0.0).then_inc(sem("stack_zeros"), 1)
                    gp.wait_ge(sem("stack_zeros"), 2 * layer + n + 1)
                gp.memset(ks[STK:STK + 2, :, :].bitcast(F32), 1.0).then_inc(sem("stack_ones"), 1)
                gp.wait_ge(sem("stack_ones"), layer + 1)

            for g in range(G):
                rstd_groups("q0", g)
            gp.wait_ge(sem("rstd_ready"), G)
            stack_rows(0)
            power(qrs[0:C, 0:4], qve[0:C, 0:4], "ctx_var", 1, "ctx_rstd")
            gp.wait_ge(sem("ctx_rstd"), 1)
            attention(0)
            for g in range(G):
                rstd_groups("x0", g)

            def cross0_power(g, which):
                lo = GT * which
                power(qrs[:, lo:lo + GT], qve[:, lo:lo + GT], f"x0_var{which}", g + 1, f"x0_rstd{which}")

            gp.wait_ge(sem("xn_ready"), G * TURN["x0"] + 1)
            add_rows(0, bB[:, :], "beta_added")
            cross0_power(0, 0)
            for g in range(G):
                if g + 1 < G:
                    cross0_power(g + 1, 0)
                    gp.wait_ge(sem("xn_ready"), G * TURN["x0"] + g + 2)
                    add_rows(g + 1, bB[:, :], "beta_added")
                for gg in ((), (0,), (1,), (2, 3))[g]:
                    cross0_power(gg, 1)
                    rstd_groups("f0", gg)
            gp.wait_ge(sem("f_mm"), 2 * FM * G)
            gp.wait_ge(sem("rstd_ready"), G * (RSTD["f0"] + 1))
            stack_rows(1)
            for g in range(G):
                rstd_groups("q1", g)
            attention(1)
            for g in range(G):
                rstd_groups("x1", g)
            gp.wait_ge(sem("we_high"), 1)
            gp.tensor_tensor(wehl[1], we, wehl[0].bitcast(F32), ALU.subtract).then_inc(sem("we_low"), 1)
            for g in range(G):
                rstd_groups("m1", g)

        @block.scalar
        def _(sc_):
            act_ = nc.scalar.activation

            def evac_T(tag, g, free=None):
                sc_.wait_ge(sem("lnT"), G * TURN[tag] + g + 1)
                if free and g >= 2:
                    sc_.wait_ge(sem(free[0]), free[1](g - 2))
                for k in range(K):
                    ins = act_(xT[:, g % 2, k, :], psum[:, k, :], ACT.Copy)
                ins.then_inc(sem("xT_ready"), 1)

            sc_.wait_ge(sem("x_loaded0"), 16)
            for dst, src in ((ctxT, d["ctxT"]), (xwkv, d["xwkv"]), (w1kv, d["w1kv"]), (w1q, d["w1q"]), (mask[:, :], d["mask"]),
                             (gB[:, :], d["g"].partition_broadcast(P)), (bB[:, :], d["b"].partition_broadcast(P)), (dmask, d["dmask"])):
                sc_.dma_start(dst, src).then_inc(sem("w_ctx"), 16)

            def context_side():
                sc_.wait_ge(sem("ctx_mm"), 1)
                act_(v1[:, :, :], psum[0:C, 6, :].rearrange("p (b n) -> p b n", b=B), ACT.Copy)
                for m in range(K):
                    ins = act_(k1T[:, m, :], psum[:, 4 + m, 0:B * C], ACT.Copy)
                ins.then_inc(sem("k1T_ready"), 1)
                sc_.wait_ge(sem("km_mm"), 1)
                for b in range(B):
                    for m in range(K):
                        ins = act_(km[:, b, m, :], psum[:, 7, C * (B * m + b):C * (B * m + b) + C], ACT.Copy)
                ins.then_inc(sem("km_ready"), 1)

            def qkv(layer):
                tag = f"q{layer}"
                for g in range(G):
                    if g == 0:
                        evac_T(tag, 0)
                    for n, u in qunits(g)[:4]:
                        if u == 3 and g + 1 < G:
                            evac_T(tag, g + 1, ("qkv_mm", lambda p: 6 * (G * layer + p + 1)))
                        sc_.wait_ge(sem("qkv_mm"), 6 * G * layer + n + 1)
                        if u >= 2:
                            sc_.wait_ge(sem(f"split_stored{layer}_{u - 2}"), 48 * (g + 1))
                        elif g >= 1:
                            sc_.wait_ge(sem(f"split_stored{layer}_{u + 2}"), 32 * g)
                        act_(hl[:, u % 2, 0, :], psum[:, 4 + n % 4, :], ACT.Identity,
                             bias=bqk[layer][:, u:u + 1]).then_inc(sem("high_ready"), 1)
                    if layer == 0 and g == 0:
                        context_side()

            def attention(layer):
                per = b_before(layer, NK)
                sc_.sem_inc(sem(f"probs_ready{layer}"), 2)
                sc_.sem_inc(sem(f"out_ready{layer}"), 2)

                def exps(head, kb):
                    sc_.wait_ge(sem(f"pv{layer}"), NK * head + kb + 1)
                    for r, (lo, hi) in enumerate(b_units(layer, kb)):
                        idx = b_before(layer, kb) + r
                        sc_.wait_ge(sem(f"scores{layer}"), per * head + idx + 1)
                        act_(probs[:, kb % 4, lo:hi], psum[:, 4 + idx % 2, lo % 512:lo % 512 + hi - lo], ACT.Exp,
                             scale=HD ** -0.5).then_inc(sem(f"probs_ready{layer}"), 1)

                def heads(i, first, last):
                    for s in range(SLOTS):
                        head = SLOTS * i + s
                        for t in range(NK):
                            if t + 1 < NK:
                                exps(head, t + 1)
                            elif not (last and s == SLOTS - 1):
                                exps(head + 1, 0)
                        sc_.wait_ge(sem(f"pv{layer}"), NK * (head + 1) + 4)
                        if not first:
                            sc_.wait_ge(sem(f"out_stored{layer}_{s}"), 64 * i)
                        act_(osb[:, s, :], psum[:, 6 + s % 2, 0:2 * P], ACT.Copy).then_inc(sem(f"out_ready{layer}"), 1)

                exps(0, 0)
                heads(0, True, False)
                with sc_.Fori(1, B * H // SLOTS - 1) as i:
                    heads(i, False, False)
                heads(B * H // SLOTS - 1, False, True)

            def ffn_weights():
                for n in range(9):
                    sc_.wait_ge(sem("wT_mm"), n + 1)
                    dst = (wgp, wup)[n // 3][:, 512 * (n % 3):512 * (n % 3) + 512] if n < 6 else at(BIG + WTS // 2 + 512 * (n - 6), 512)
                    act_(dst, psum[:, n % 4, :], ACT.Copy).then_inc(sem("wT_ready"), 1)

            def cross0():
                def rest(g):
                    sc_.wait_ge(sem("x0_T2"), g + 1)
                    for k in range(K):
                        ins = act_(qT[:, k, GN * (g % 2):GN * (g % 2) + GN], psum[:, 4 + k, :], ACT.Identity, scale=gcol[:, k:k + 1], bias=bcol[:, k:k + 1])
                    ins.then_inc(sem("x0_affine"), 1)
                evac_T("x0", 0)
                for g in range(G):
                    if g + 1 < G:
                        evac_T("x0", g + 1, ("x0_q", lambda p: p + 1))
                    rest(g)
                    for gg in (g - 1, g) if g % 2 else ():
                        sc_.wait_ge(sem("x0_T3"), gg + 1)
                        for k in range(K):
                            ins = act_(attT[:, k, :], psum[:, 4 + k, :], ACT.Copy)
                        ins.then_inc(sem("x0_attT"), 1)

            def ffn():
                for g in range(G):
                    sc_.wait_ge(sem("f_T"), g + 1)
                    for k in range(K):
                        ins = act_(xqT[:, k, GN * g:GN * g + GN], psum[:, 2 * (g % 2) + k, :], ACT.Copy)
                    ins.then_inc(sem("xqT_ready"), 1)

                def split(step):
                    g = step % G
                    if step >= 2:
                        sc_.wait_ge(sem("f_mm"), FM * (step - 1))
                    act_(xhl[:, step % 2, 0, :, :], xqT[:, :, GN * g:GN * g + GN], ACT.Copy).then_inc(sem("f_high"), 1)

                sc_.wait_ge(sem("xqT_ready"), G)
                split(0)
                for n in range(2 * FM * G):
                    step, m = divmod(n, FM)
                    g = step % G
                    if m == 0 and step + 1 < 2 * G:
                        split(step + 1)
                    sc_.wait_ge(sem("f_mm"), n + 1)
                    if step >= G:
                        sc_.wait_ge(sem("qup_ready"), g + 1)
                    act_(act[:, m, GN * g:GN * g + GN], psum[:, n % 6, :], ACT.Copy).then_inc(sem("f_evac"), 1)
                for m in range(FM):
                    sc_.wait_ge(sem("qgate_ready"), m + 1)
                    if m + 1 < FM:
                        act_(qgate[:, m + 1, :], act[:, m + 1, :], ACT.Identity, scale=sc[:, 21:22]).then_inc(sem("qgate_ready"), 1)
                    act_(act[:, m, :], qgate[:, m, :], ACT.Sigmoid, scale=sc[:, 20:21]).then_inc(sem("sigmoid_ready"), 1)
                sc_.wait_ge(sem("p_scaled"), 1)
                for m in range(FM):
                    act_(qgate[:, m, :], act[:, m, :], ACT.Identity, scale=sc[:, 26:27]).then_inc(sem("qp_ready"), 1)

            def cross1():
                sc_.wait_ge(sem("w_experts"), 16)
                sc_.wait_ge(sem("proj_done"), 4 * G)
                act_(wehl[0], we, ACT.Copy).then_inc(sem("we_high"), 1)
                for g in range(G):
                    if g == 0:
                        evac_T("x1", 0)
                    if g + 1 < G:
                        evac_T("x1", g + 1, ("x1_scores", lambda p: p + 1))
                    sc_.wait_ge(sem("x1_max"), g + 1)
                    for t in range(GT):
                        ins = act_(pm[:, C * t:C * t + C], psum[:, 2, C * t:C * t + C], ACT.Exp, scale=D ** -0.5,
                                   bias=qve[:, t:t + 1], accum_out=qrs[:, t:t + 1])
                    ins.then_inc(sem("x1_exp"), 1)
                    sc_.wait_ge(sem("x1_T2"), g + 1)
                    act_(pT[0:C, :], psum[0:C, 3, :], ACT.Copy).then_inc(sem("x1_pT"), 1)

            def experts():
                def turned(g):
                    sc_.wait_ge(sem("lnT"), G * TURN["m1"] + g + 1)
                    if g >= 2:
                        sc_.wait_ge(sem("m1_mm"), 16 * (g - 1))
                    for k in range(K):
                        act_(xhl[:, g % 2, 0, k, :], psum[:, k, :], ACT.Copy)
                    for k in range(K):
                        ins = act_(x32[:, g % 2, k, :], psum[:, k, :], ACT.Copy)
                    ins.then_inc(sem("xT_ready"), 1)

                def routing(g):
                    sc_.wait_ge(sem("m1_shift"), g + 1)
                    act_(ex, ex, ACT.Exp).then_inc(sem("m1_exp"), 1)
                    sc_.wait_ge(sem("m1_T2"), g + 1)
                    act_(mwT[0:E, :], psum[0:E, 3, :], ACT.Copy).then_inc(sem("m1_mwT"), 1)

                turned(0)
                turned(1)
                routing(0)
                for g in range(G):
                    if g + 1 < G:
                        routing(g + 1)
                    if g + 2 < G:
                        turned(g + 2)

            qkv(0)
            attention(0)
            ffn_weights()
            cross0()
            ffn()
            qkv(1)
            attention(1)
            cross1()
            experts()

        @block.tensor
        def _(pe):
            mm = nc.tensor.matmul

            def transpose_rows(tag, g):
                pe.wait_ge(sem("xn_ready"), G * TURN[tag] + g + 1)
                if g >= 1:
                    pe.wait_ge(sem("xT_ready"), G * TURN[tag] + g)
                for k in range(K):
                    for t in range(GT):
                        ins = nc.tensor.transpose(psum[:, k, P * t:P * t + P], xn[:, g % 2, t, P * k:P * k + P], ident[:, :])
                ins.then_inc(sem("lnT"), 1)

            pe.wait_ge(sem("const_loaded"), 16)

            def context_side():
                pe.wait_ge(sem("qkv_drained"), 6)
                pe.wait_ge(sem("w_ctx"), 16 * 8)
                for b in range(B):
                    cols = slice(C * b, C * b + C)
                    for k in range(K):
                        mm(psum[0:C, 2 + b, :], ctxT[:, k, cols], xwkv[:, k, :], start=(k == 0), stop=(k == K - 1))
                    for k in range(K):
                        mm(psum[0:C, 6, D * b:D * b + D], ctxT[:, k, cols], w1kv[:, k, D:2 * D], start=(k == 0), stop=(k == K - 1))
                for m in range(K):
                    for k in range(K):
                        ins = mm(psum[:, 4 + m, 0:B * C], w1kv[:, k, P * m:P * m + P], ctxT[:, k, :], start=(k == 0), stop=(k == K - 1))
                ins.then_inc(sem("ctx_mm"), 1)
                pe.wait_ge(sem("k1T_ready"), 1)
                for m in range(K):
                    for k in range(K):
                        ins = mm(psum[:, 7, B * C * m:B * C * (m + 1)], w1q[:, k, P * m:P * m + P], k1T[:, k, :], start=(k == 0), stop=(k == K - 1))
                ins.then_inc(sem("km_mm"), 1)
                pe.wait_ge(sem("km_ready"), 1)

            def qkv(layer):
                tag = f"q{layer}"
                transpose_rows(tag, 0)
                if layer == 0:
                    pe.wait_ge(sem("w_rotated"), 1)
                else:
                    pe.wait_ge(sem("w_qkv1"), 16 * 3)
                for g in range(G):
                    pe.wait_ge(sem("xT_ready"), G * TURN[tag] + g + 1)
                    for n, u in qunits(g):
                        if u == 3 and g + 1 < G:
                            transpose_rows(tag, g + 1)
                        bank = 4 + n % 4
                        if n >= 4:
                            pe.wait_ge(sem("qkv_drained"), 6 * G * layer + n - 3)
                        if u < 4:
                            for k in range(K):
                                ins = mm(psum[:, bank, :], wqk[:, k, P * u:P * u + P], xT[:, g % 2, k, :],
                                         start=(k == 0), stop=(k == K - 1))
                        else:
                            for i in range(2):
                                t = 2 * (u - 4) + i
                                for k in range(K):
                                    ins = mm(psum[:, bank, D * i:D * i + D], xT[:, g % 2, k, P * t:P * t + P], wv[:, k, :],
                                             start=(k == 0), stop=(k == K - 1))
                        ins.then_inc(sem("qkv_mm"), 1)
                    if layer == 0 and g == 0:
                        context_side()

            def context_products():
                pe.wait_ge(sem("ctx_kv"), 1)
                pe.wait_ge(sem("wT_ready"), 9)
                pe.wait_ge(sem("wT_low"), 6)
                for b in range(B):
                    for m in range(K):
                        ins = mm(psum[:, 2 * b + m, 0:D + H], kvn[0:C, b, P * m:P * m + P], vext[0:C, b, :], start=True, stop=True)
                ins.then_inc(sem("kv_mm"), 1)

            def attention(layer):
                per = b_before(layer, NK)
                pe.wait_ge(sem("ones_ready"), layer + 1)
                if layer == 0:
                    pe.wait_ge(sem("ctx_kv"), 1)
                pe.sem_inc(sem(f"pv{layer}"), 4)
                if layer == 0:
                    pe.wait_ge(sem("w_rest"), 16 * W_REST)
                pe.wait_ge(sem("stack_ones"), layer + 1)
                pe.wait_ge(sem("qkv_drained"), 6 * G * layer + 6 * G)

                def max_scores(head, s, use, qt, ring=True):
                    if qt == 0:
                        pe.wait_ge(sem(f"stack_loaded{layer}_{s}"), 64 * use + 64)
                    if ring:
                        pe.wait_ge(sem(f"max_taken{layer}"), NK * head + qt - 1)
                    cols = a_cols(layer, qt)
                    q = qs[0:STK, s, P * qt:P * qt + P]
                    for half in range((cols + 511) // 512):
                        lo, hi = 512 * half, min(cols, 512 * half + 512)
                        diag = layer == 1 and hi == cols
                        bank = 2 * (qt % 2) + half
                        ins = mm(psum[:, bank, 0:hi - lo], q, ks[0:STK, s, lo:hi], start=True, stop=not diag)
                        if diag:
                            ins = mm(psum[:, bank, hi - lo - P:hi - lo], identb[:, :], causal[:, 0, :], start=False, stop=True)
                    ins.then_inc(sem(f"max_scores{layer}"), 1)

                def turn_max(head, par):
                    pe.wait_ge(sem("max_split"), B * H * layer + head + 1)
                    pe.wait_ge(sem(f"out_ready{layer}"), head + 1)
                    nc.tensor.transpose(psum[0:2 * NK, 6 + par, 384:512], tin[:, :], ident[:, :]).then_inc(sem("max_turned"), 1)

                def scores(head, s, use, kb):
                    if kb == 0:
                        pe.wait_ge(sem(f"max_loaded{layer}_{s}"), 32 * use + 32)
                    k = ks[0:STKM, s, P * kb:P * kb + P]
                    for r, (lo, hi) in enumerate(b_units(layer, kb)):
                        idx = b_before(layer, kb) + r
                        pe.wait_ge(sem(f"probs_ready{layer}"), per * head + idx + 1)
                        diag = layer == 1 and r == 0
                        bank, off = 4 + idx % 2, lo % 512
                        ins = mm(psum[:, bank, off:off + hi - lo], k, qs[0:STKM, s, lo:hi], start=True, stop=not diag)
                        if diag:
                            ins = mm(psum[:, bank, off:off + P], identb[:, :], causal[:, 1, :], start=False, stop=True)
                        ins.then_inc(sem(f"scores{layer}"), 1)

                def values(head, s, kb):
                    if kb == 0:
                        pe.wait_ge(sem("values_copied"), B * H * layer + head + 1)
                        pe.wait_ge(sem(f"out_ready{layer}"), head + 1)
                    pe.wait_ge(sem(f"probs_ready{layer}"), per * head + b_before(layer, kb + 1) + 2)
                    for j in range(4):
                        qt = pv_blocks(layer, kb, j)
                        if not qt:
                            continue
                        lo = 0 if len(qt) == 2 else P
                        rhs = probs[:, kb % 4, :].rearrange("p (q c) -> p q c", q=NK)[:, qt[0]:qt[-1] + 1:max(1, qt[-1] - qt[0]), :]
                        dst = psum[32 * j:32 * j + VW, 6 + s % 2, lo:2 * P].rearrange("p (q c) -> p q c", c=P)
                        last = kb == NK - 1 if layer == 0 else kb == NK - 1 - j
                        ins = mm(dst, vs[:, s, kb, :], rhs, start=(kb == 0), stop=last, skip_group_check=True)
                    ins.then_inc(sem(f"pv{layer}"), 1)

                for a in range(LEAD):
                    max_scores(a // NK, a // NK, 0, a % NK, ring=a >= 2)
                    if a == NK + 1:
                        turn_max(0, 0)
                scores(0, 0, 0, 0)

                def heads(i, last):
                    for s in range(SLOTS):
                        head = SLOTS * i + s
                        for t in range(NK):
                            dh, r = divmod(t + LEAD, NK)
                            if not (last and s + dh >= SLOTS):
                                max_scores(head + dh, (s + dh) % SLOTS, i + (s + dh) // SLOTS, r)
                            if t + 1 < NK:
                                scores(head, s, i, t + 1)
                            elif not (last and s == SLOTS - 1):
                                scores(head + 1, (s + 1) % SLOTS, i + (s + 1) // SLOTS, 0)
                            values(head, s, t)
                            if t == 2 and not (last and s == SLOTS - 1):
                                turn_max(head + 1, (s + 1) % 2)

                with pe.Fori(0, B * H // SLOTS - 1) as i:
                    heads(i, False)
                heads(B * H // SLOTS - 1, True)

            def project(layer):
                if layer == 0:
                    pe.wait_ge(sem("kvbd_ready"), 1)
                else:
                    pe.wait_ge(sem("w_out1"), 16 * 2)

                def spread(c):
                    b, half = divmod(c, 2)
                    pe.wait_ge(sem("sums_inverted"), 2 * layer + (half + 1 if b == 0 else 2))
                    for k in range(K):
                        n = 2 * c + k
                        if n >= 4:
                            pe.wait_ge(sem("attn_ready"), 4 * B * layer + n - 3)
                        mm(psum[:, n % 4, :], pick[:, b, P * k:P * k + P], qs[0:2 * B * H, 0, 512 * half:512 * half + 512],
                           start=True, stop=True).then_inc(sem("sums_spread"), 1)

                spread(0)
                spread(1)
                for u in range(2 * G):
                    b = u // G
                    if u % 2 == 0 and u // 2 + 2 < G:
                        spread(u // 2 + 2)
                    pe.wait_ge(sem("attn_ready"), 4 * B * layer + 2 * (u // 2) + 2)
                    if u >= 4:
                        pe.wait_ge(sem("proj_drained"), 2 * G * layer + u - 3)
                    for i in range(2):
                        kb = (2 * u + i) % NK
                        for k in range(K):
                            ins = mm(psum[:, 4 + u % 4, D * i:D * i + D], num[:, b, k, P * kb:P * kb + P], wo[:, k, :],
                                     start=(k == 0), stop=(k == K - 1))
                    ins.then_inc(sem("proj_done"), 1)

            def ffn_weights():
                pe.wait_ge(sem("w_dequant"), 4)
                pe.wait_ge(sem("max_taken0"), NK * B * H)
                for n in range(9):
                    if n >= 4:
                        pe.wait_ge(sem("wT_low"), n - 3)
                    for c in range(4):
                        i = 4 * (n % 3) + c
                        if n < 6:
                            k, m = divmod(i, FM)
                            src = (rawg if n < 3 else rawu)[:, m, P * k:P * k + P]
                        else:
                            m, k = divmod(i, K)
                            src = rawd[:, k, P * m:P * m + P]
                        ins = nc.tensor.transpose(psum[:, n % 4, P * c:P * c + P], src, ident[:, :])
                    ins.then_inc(sem("wT_mm"), 1)

            def rows_times(g, w, bank, name, src, cols=D):
                for t in range(GT):
                    for k in range(K):
                        ins = mm(psum[:, bank + t // 2, D * (t % 2):D * (t % 2) + cols], src[:, k, P * t:P * t + P], w[:, k, 0:cols],
                                 start=(k == 0), stop=(k == K - 1))
                ins.then_inc(sem(name), 1)

            def cross0():
                def queries(g):
                    pe.wait_ge(sem("xT_ready"), G * TURN["x0"] + g + 1)
                    if g >= 1:
                        pe.wait_ge(sem("x0_qn"), g)
                    rows_times(g, xwq, 2, "x0_q", xT[:, g % 2])

                def turn(src, done):
                    for k in range(K):
                        for t in range(GT):
                            ins = nc.tensor.transpose(psum[:, 4 + k, P * t:P * t + P], src[:, t, P * k:P * k + P], ident[:, :])
                    ins.then_inc(sem(done), 1)

                transpose_rows("x0", 0)
                queries(0)
                for g in range(G):
                    b = g // 2
                    if g + 1 < G:
                        transpose_rows("x0", g + 1)
                    pe.wait_ge(sem("x0_qn"), g + 1)
                    if g >= 2:
                        pe.wait_ge(sem("x0_attT"), 2 * (g // 2))
                    elif g == 1:
                        pe.wait_ge(sem("x0_affine"), 1)
                    if g == 3:
                        pe.wait_ge(sem("x0_affine"), 3)
                    turn(qn[:, g % 2], "x0_T2")
                    if g + 1 < G:
                        queries(g + 1)
                    if g % 2 == 0:
                        continue
                    pe.wait_ge(sem("x0_qT"), g + 1)
                    if b:
                        pe.wait_ge(sem("x0_y"), 2 * b)
                    for half in range(2):
                        if half and g + 1 < G:
                            pe.wait_ge(sem("xT_ready"), G * TURN["x0"] + g + 2)
                        for i in range(NK):
                            nn = NK * half + i
                            bank, lo = kv_place(half, i)
                            for j in range(2):
                                for k in range(K):
                                    ins = mm(psum[64 * j:64 * j + 64, bank, lo + KV * k:lo + KV * k + KV], qT[:, k, nn:S:HD],
                                             kvbd[:, b, k, j, :], start=True, stop=True)
                        ins.then_inc(sem("x0_kv"), 1)
                    pe.wait_ge(sem("x0_att"), 2 * b + 2)
                    for gg in (g - 1, g):
                        if gg % 2:
                            pe.wait_ge(sem("x0_attT"), gg)
                            pe.wait_ge(sem("x0_y"), gg)
                        turn(att[:, GT * (gg % 2):GT * (gg % 2) + GT], "x0_T3")
                        pe.wait_ge(sem("x0_attT"), gg + 1)
                        rows_times(gg, xwd, 6, "x0_out", attT)

            def global_max(n):
                pe.wait_ge(sem("gm_col"), n + 1)
                mm(psum[0:1, 7, 0:P], sc[:, 0:1], ident[:, :], start=True, stop=True).then_inc(sem("gm_row"), 1)
                pe.wait_ge(sem("gm_one"), n + 1)
                mm(psum[:, 7, 256:257], ones[0:1, :], sc[0:1, 1:2], start=True, stop=True).then_inc(sem("gm_all"), 1)

            def ffn():
                global_max(0)
                for g in range(G):
                    pe.wait_ge(sem("xq_ready"), g + 1)
                    if g >= 2:
                        pe.wait_ge(sem("xqT_ready"), g - 1)
                    for k in range(K):
                        for t in range(GT):
                            ins = nc.tensor.transpose(psum[:, 2 * (g % 2) + k, P * t:P * t + P],
                                                      xq[:, GT * g + t, P * k:P * k + P], ident[:, :])
                    ins.then_inc(sem("f_T"), 1)
                pe.wait_ge(sem("xqT_ready"), G)
                for n in range(2 * FM * G):
                    step, m = divmod(n, FM)
                    if m == 0:
                        pe.wait_ge(sem("f_low"), step + 1)
                    if n >= 6:
                        pe.wait_ge(sem("f_evac"), n - 5)
                    if n == FM * G + 4:
                        global_max(1)
                    w = wuT if n < FM * G else wgT
                    terms = [(k, xp, wp) for k in range(K) for xp, wp in ((0, 0), (0, 1), (1, 0))]
                    for i, (k, xp, wp) in enumerate(terms):
                        ins = mm(psum[:, n % 6, :], w[:, wp, k, P * m:P * m + P], xhl[:, step % 2, xp, k, :],
                                 start=(i == 0), stop=(i == len(terms) - 1))
                    ins.then_inc(sem("f_mm"), 1)
                for n in (2, 3, 4):
                    global_max(n)
                for u in range(2 * G):
                    pe.wait_ge(sem("q3_ready"), u // 2 + 1)
                    if u >= 4:
                        pe.wait_ge(sem("down_drained"), u - 3)
                    for i in range(2):
                        t = 2 * u + i
                        for m in range(FM):
                            ins = mm(psum[:, u % 4, D * i:D * i + D], act[:, m, P * t:P * t + P], wdT[:, m, :],
                                     start=(m == 0), stop=(m == FM - 1))
                    ins.then_inc(sem("down_mm"), 1)

            def cross1():
                transpose_rows("x1", 0)
                for g in range(G):
                    b = g // 2
                    if g + 1 < G:
                        transpose_rows("x1", g + 1)
                    pe.wait_ge(sem("xT_ready"), G * TURN["x1"] + g + 1)
                    if g >= 1:
                        pe.wait_ge(sem("x1_exp"), g)
                    for t in range(GT):
                        for k in range(K):
                            ins = mm(psum[:, 2, C * t:C * t + C], xT[:, g % 2, k, P * t:P * t + P], km[:, b, k, :],
                                     start=(k == 0), stop=(k == K - 1))
                    ins.then_inc(sem("x1_scores"), 1)
                    pe.wait_ge(sem("x1_exp"), g + 1)
                    if g >= 1:
                        pe.wait_ge(sem("x1_pT"), g)
                    for t in range(GT):
                        ins = nc.tensor.transpose(psum[0:C, 3, P * t:P * t + P], pm[:, C * t:C * t + C], ident[:, :])
                    ins.then_inc(sem("x1_T2"), 1)
                    pe.wait_ge(sem("x1_pT"), g + 1)
                    if g >= 1:
                        pe.wait_ge(sem("x1_added"), g)
                    for t in range(GT):
                        ins = mm(psum[:, 6 + t // 2, D * (t % 2):D * (t % 2) + D], pT[0:C, P * t:P * t + P], v1[0:C, b, :],
                                 start=True, stop=True)
                    ins.then_inc(sem("x1_out"), 1)

            def experts():
                def logits(g):
                    pe.wait_ge(sem("xT_ready"), G * TURN["m1"] + g + 1)
                    for t in range(GT):
                        for k in range(K):
                            ins = mm(psum[:, 2, E * t:E * t + E], x32[:, g % 2, k, P * t:P * t + P], rw[:, k, :],
                                     start=(k == 0), stop=(k == K - 1))
                    ins.then_inc(sem("m1_logits"), 1)

                def weights_to_rows(g):
                    pe.wait_ge(sem("m1_mw"), g + 1)
                    for t in range(GT):
                        ins = nc.tensor.transpose(psum[0:E, 3, P * t:P * t + P], mw[:, t, :], ident[:, :])
                    ins.then_inc(sem("m1_T2"), 1)

                def bias(g):
                    pe.wait_ge(sem("m1_mwT"), g + 1)
                    for t in range(GT):
                        ins = mm(psum[:, 2 + t // 2, D * (t % 2):D * (t % 2) + D], mwT[0:E, P * t:P * t + P], eb[:, :],
                                 start=True, stop=True)
                    ins.then_inc(sem("m1_bias"), 1)

                def expert_pairs(g, t):
                    for c in range(E // 2):
                        n = 16 * g + 4 * t + c
                        if n >= 4:
                            pe.wait_ge(sem("m1_added"), n - 3)
                        cols = slice(2 * D * c, 2 * D * c + 2 * D)
                        rows = slice(P * t, P * t + P)
                        terms = [(k, xp, wp) for k in range(K) for xp, wp in ((0, 0), (0, 1), (1, 0))]
                        for i, (k, xp, wp) in enumerate(terms):
                            ins = mm(psum[:, 4 + n % 4, :], xhl[:, g % 2, xp, k, rows], wehl[wp][:, k, cols],
                                     start=(i == 0), stop=(i == len(terms) - 1))
                        ins.then_inc(sem("m1_mm"), 1)

                transpose_rows("m1", 0)
                logits(0)
                pe.wait_ge(sem("m1_low"), 1)
                transpose_rows("m1", 1)
                weights_to_rows(0)
                bias(0)
                pe.wait_ge(sem("we_low"), 1)
                for g in range(G):
                    pe.wait_ge(sem("m1_low"), g + 1)
                    expert_pairs(g, 0)
                    if g + 1 < G:
                        pe.wait_ge(sem("m1_bias_added"), g + 1)
                        logits(g + 1)
                    expert_pairs(g, 1)
                    expert_pairs(g, 2)
                    if g + 1 < G:
                        weights_to_rows(g + 1)
                    expert_pairs(g, 3)
                    if g + 1 < G:
                        bias(g + 1)
                    if g + 2 < G:
                        pe.wait_ge(sem("m1_low"), g + 2)
                        transpose_rows("m1", g + 2)

            qkv(0)
            attention(0)
            ffn_weights()
            context_products()
            project(0)
            cross0()
            ffn()
            qkv(1)
            attention(1)
            project(1)
            cross1()
            experts()

        @block.vector
        def _(ve):
            v = nc.vector
            V = Steps(ve, sem("dve_step"))

            def group_stats(g, tag):
                V.sync()
                for t in range(GT):
                    ins = v.bn_stats(stats[:, t, :], x[:, GT * g + t, :])
                V(ins)
                V.sync()
                for t in range(GT):
                    ins = v.bn_aggr(mv[:, GT * g + t, :], stats[:, t, :])
                V(ins)
                V.sync()
                v.tensor_scalar(veps[:, GT * g:GT * g + GT], mv[:, GT * g:GT * g + GT, 1], LN_EPS, None, ALU.add)\
                    .then_inc(sem("var_ready"), 1)

            def normalise(g, tag):
                ve.wait_ge(sem("rstd_ready"), G * RSTD[tag] + g + 1)
                if g >= 2:
                    ve.wait_ge(sem("lnT"), G * TURN[tag] + g - 1)
                for t in range(GT):
                    tt = GT * g + t
                    ins = v.tensor_scalar(xn[:, g % 2, t, :], x[:, tt, :], mv[:, tt, 0:1], rstd[:, tt:tt + 1],
                                          ALU.subtract, ALU.mult)
                ins.then_inc(sem("xn_ready"), 1)

            V(v.memset(vext[:, :, D:D + H], 1.0))
            ve.wait_ge(sem("x_loaded0"), 16)
            group_stats(0, "q0")

            ve.wait_ge(sem("w_qkv0"), 16 * 10)
            for k in range(K):
                v.tensor_tensor(wswap[:, k, :], wswap[:, k, :], sinr, ALU.mult)
                v.tensor_tensor(wqk[:, k, :], wqk[:, k, :], cosr, ALU.mult)
            v.tensor_tensor(bswap, bswap, sincol, ALU.mult)
            V(v.tensor_tensor(bqk[0][:, :], bqk[0][:, :], coscol, ALU.mult))
            V.sync()
            v.tensor_tensor(bqk[0][:, :], bqk[0][:, :], bswap, ALU.add)
            v.tensor_tensor(wqk[:, :, :], wqk[:, :, :], wswap, ALU.add).then_inc(sem("w_rotated"), 1)

            def context_side():
                ve.wait_ge(sem("w_ctx"), 16 * 8)
                ve.wait_ge(sem("ctx_mm"), 1)
                for i in range(2 * B):
                    ins = v.bn_stats(qstat[0:C, i, :], psum[0:C, 2 + i // 2, D * (i % 2):D * (i % 2) + D])
                V(ins)
                V.sync()
                for i in range(2 * B):
                    ins = v.bn_aggr(qmv[0:C, i, :], qstat[0:C, i, :])
                V(ins)
                V.sync()
                v.tensor_scalar(qve[0:C, 0:4], qmv[0:C, 0:4, 1], X_EPS, None, ALU.add).then_inc(sem("ctx_var"), 1)
                ve.wait_ge(sem("ctx_rstd"), 1)
                for i in range(2 * B):
                    ins = v.tensor_scalar(kvn[0:C, i // 2, D * (i % 2):D * (i % 2) + D], psum[0:C, 2 + i // 2, D * (i % 2):D * (i % 2) + D],
                                          qmv[0:C, i, 0:1], qrs[0:C, i:i + 1], ALU.subtract, ALU.mult)
                V(ins)
                for row, op in ((gB, ALU.mult), (bB, ALU.add)):
                    V.sync()
                    for i in range(2 * B):
                        part = kvn[0:C, i // 2, D * (i % 2):D * (i % 2) + D]
                        ins = v.tensor_tensor(part, part, row[0:C, :], op)
                    V(ins)
                V.sync()
                for b in range(B):
                    v.tensor_scalar(vext[0:C, b, 0:D], kvn[0:C, b, D:2 * D], mask[:, b:b + 1], None, ALU.mult)
                    ins = v.tensor_scalar(kvn[0:C, b, 0:D], kvn[0:C, b, 0:D], 0.0, X_EPS, ALU.max, ALU.add)
                V(ins)
                V.sync()
                for b in range(B):
                    ins = v.tensor_scalar(kvn[0:C, b, 0:D], kvn[0:C, b, 0:D], mask[:, b:b + 1], None, ALU.mult)
                ins.then_inc(sem("ctx_kv"), 1)

            def qkv(layer):
                tag = f"q{layer}"
                v.memset(vs[:, :, :, HD:VW], 1.0).then_inc(sem("ones_ready"), 1)
                if layer == 1:
                    ve.wait_ge(sem("w_qkv1"), 16 * 3)
                else:
                    normalise(0, tag)
                    for g in range(1, G):
                        ve.wait_ge(sem(f"x_loaded{g}"), 16)
                        group_stats(g, "q0")
                for g in range(G):
                    b = g // 2
                    for n, u in qunits(g):
                        if u == 1 and g + 1 < G:
                            normalise(g + 1, tag)
                        bank = 4 + n % 4
                        if u < 4:
                            ve.wait_ge(sem("high_ready"), 4 * G * layer + 4 * g + u + 1)
                            ins = v.scalar_tensor_tensor(out=hl[:, u % 2, 1, :], in0=psum[:, bank, :], scalar=bqk[layer][:, u:u + 1],
                                                         in1=hl[:, u % 2, 0, :].bitcast(F32), op0=ALU.add, op1=ALU.subtract)
                        else:
                            ve.wait_ge(sem("qkv_mm"), 6 * G * layer + n + 1)
                            for i in range(2):
                                kb = (GT * g + 2 * (u - 4) + i) % NK
                                ins = v.tensor_tensor(vall[:, b, :, kb, :], psum[:, bank, D * i:D * i + D].rearrange("p (h d) -> p h d", h=H),
                                                      bv.rearrange("p (h d) -> p h d", h=H), ALU.add)
                        ins.then_inc(sem("qkv_drained"), 1)
                        if layer == 0 and n >= 16:
                            ffn_weights(*divmod(n - 16, WSTEPS))
                    if layer == 0 and g == 0:
                        context_side()

            WSTEPS = 4

            def ffn_weights(step, part):
                n = 144 // WSTEPS
                rows = slice(n * part, n * part + n)
                if step == 0:
                    ve.wait_ge(sem("w_ffn"), 16)
                    V(v.tensor_reduce(wsc[:, rows], raw[:, rows, :], AX, ALU.max, apply_absolute_value=True))
                elif step == 1:
                    if part == 0:
                        V.sync()
                        V(v.tensor_scalar(wsc, wsc, 1.0 / 7.0, TINY, ALU.mult, ALU.max))
                        V.sync()
                        V(v.reciprocal(wrc, wsc))
                        V.sync()
                    V(v.tensor_tensor(wint[:, rows, :], raw[:, rows, :], bc(wrc[:, rows], QB, 2), ALU.mult))
                else:
                    V.sync()
                    v.tensor_tensor(raw[:, rows, :], wint[:, rows, :], bc(wsc[:, rows], QB, 2), ALU.mult).then_inc(sem("w_dequant"), 1)

            def context_products():
                ve.wait_ge(sem("kv_mm"), 1)
                for b in range(B):
                    for m in range(K):
                        for j in range(2):
                            for lo, n, w, dst in ((P * m, P, HD, kvbd[:, b, m, j, 0:4 * HD]), (D + 8 * m, 8, 1, kvbd[:, b, m, j, 4 * HD:KV])):
                                pick_heads = lambda ap: ap.rearrange("p (t j e) -> p t j e", j=2, e=w)[:, :, j, :]
                                ins = v.tensor_tensor(dst.rearrange("p (t e) -> p t e", e=w), pick_heads(psum[:, 2 * b + m, lo:lo + n]),
                                                      pick_heads(dmask[:, m, lo:lo + n]), ALU.mult)
                ins.then_inc(sem("kvbd_ready"), 1)

            def attention(layer):
                def take_max(head, par, qt):
                    ve.wait_ge(sem(f"max_scores{layer}"), NK * head + qt + 1)
                    v.tensor_reduce(nmax[:, par, qt:qt + 1], pflat[:, S * (qt % 2):S * (qt % 2) + a_cols(layer, qt)], AX, ALU.max,
                                    negate=True).then_inc(sem(f"max_taken{layer}"), 1)

                def split_max(head, par):
                    ve.wait_ge(sem(f"max_taken{layer}"), NK * (head + 1))
                    v.tensor_copy(tin[:, 0:NK].bitcast(F32R), nmax[:, par, :]).then_inc(sem("max_high"), 1)
                    ve.wait_ge(sem("max_high"), B * H * layer + head + 1)
                    v.tensor_tensor(tin[:, NK:2 * NK].bitcast(F32R), nmax[:, par, :], tin[:, 0:NK], ALU.subtract)\
                        .then_inc(sem("max_split"), 1)

                def max_to_rows(head, par):
                    ve.wait_ge(sem("max_turned"), B * H * layer + head + 1)
                    v.tensor_copy(trow[:, :], psum[0:2 * NK, 6 + par, 384:512]).then_inc(sem("max_rows"), 1)

                def heads(i, first):
                    for s in range(SLOTS):
                        head = SLOTS * i + s
                        for r in range(NK):
                            take_max(head, s % 2, r)
                            if r == 1 and not (first and s == 0):
                                max_to_rows(head - 1, (s + 1) % 2)
                        split_max(head, s % 2)
                        if first and layer == 0:
                            ffn_weights(2, s)

                heads(0, True)
                with ve.Fori(1, B * H // SLOTS) as i:
                    heads(i, False)
                max_to_rows(B * H - 1, 1)

            def weights_low():
                for n in range(6):
                    ve.wait_ge(sem("wT_ready"), n + 1)
                    w, lo = (wgp, wup)[n // 3], 512 * (n % 3)
                    v.tensor_tensor(w[:, K * FF + lo:K * FF + lo + 512], psum[:, n % 4, :], w[:, lo:lo + 512].bitcast(F32),
                                    ALU.subtract).then_inc(sem("wT_low"), 1)

            def project(layer, nxt):
                ve.wait_ge(sem(f"sums_loaded{layer}"), 16)
                if layer == 0:
                    V(v.tensor_copy(pick[:, :, :], picked[:, :, :]))
                for half in range(2):
                    for q in range(2):
                        rows = den[0:B * H, 512 * half + 256 * q:512 * half + 256 * (q + 1)]
                        ins = v.reciprocal(rows, rows)
                    V(ins)
                    V.sync()
                    rows, high = den[0:B * H, 512 * half:512 * half + 512], qs[0:B * H, 0, 512 * half:512 * half + 512]
                    V(v.tensor_copy(high, rows))
                    V.sync()
                    v.tensor_tensor(qs[B * H:2 * B * H, 0, 512 * half:512 * half + 512], rows, high.bitcast(F32), ALU.subtract)\
                        .then_inc(sem("sums_inverted"), 1)

                def divide(c):
                    b, half = divmod(c, 2)
                    ve.wait_ge(sem(f"attended_loaded{layer}_{b}"), 16 * K)
                    for k in range(K):
                        n = 2 * c + k
                        ve.wait_ge(sem("sums_spread"), 4 * B * layer + n + 1)
                        part = num[:, b, k, 512 * half:512 * half + 512]
                        v.tensor_tensor(part, part, psum[:, n % 4, :], ALU.mult).then_inc(sem("attn_ready"), 1)

                divide(0)
                divide(1)
                for u in range(2 * G):
                    if u % 2 == 0 and u // 2 + 2 < G:
                        divide(u // 2 + 2)
                    ve.wait_ge(sem("proj_done"), 2 * G * layer + u + 1)
                    ve.wait_ge(sem("bias_added"), G * layer + u // 2 + 1)
                    ins = v.tensor_tensor(x[:, 2 * u:2 * u + 2, :], psum[:, 4 + u % 4, :].rearrange("p (t n) -> p t n", t=2),
                                          x[:, 2 * u:2 * u + 2, :], ALU.add)
                    ins.then_inc(sem("proj_drained"), 1)
                    if u % 2:
                        ve.wait_ge(sem("proj_drained"), 2 * G * layer + u + 1)
                        group_stats(u // 2, nxt)
                    if u == 5:
                        normalise(0, nxt)

            def ffn_rows(g):
                ve.wait_ge(sem("rstd_ready"), G * RSTD["f0"] + g + 1)
                for t in range(GT * g, GT * g + GT):
                    ins = v.tensor_scalar(xq[:, t, :], x[:, t, :], mv[:, t, 0:1], rstd[:, t:t + 1], ALU.subtract, ALU.mult)
                V(ins)
                V.sync()
                V(v.tensor_reduce(am[:, g:g + 1], at(1024 * g, 1024), AX, ALU.max, apply_absolute_value=True))

            def cross0(nxt):
                def query_stats(g):
                    ve.wait_ge(sem("x0_q"), g + 1)
                    row_stats(lambda t: psum[:, 2 + t // 2, D * (t % 2):D * (t % 2) + D], 0, "x0_var0")

                def row_stats(rows, lo, done):
                    for t in range(GT):
                        ins = v.bn_stats(qstat[:, t, :], rows(t))
                    V(ins)
                    V.sync()
                    for t in range(GT):
                        ins = v.bn_aggr(qmv[:, lo + t, :], qstat[:, t, :])
                    V(ins)
                    V.sync()
                    v.tensor_scalar(qve[:, lo:lo + GT], qmv[:, lo:lo + GT, 1], X_EPS, None, ALU.add).then_inc(sem(done), 1)

                def query_norm(g):
                    ve.wait_ge(sem("x0_rstd0"), g + 1)
                    if g >= 2:
                        ve.wait_ge(sem("x0_T2"), g - 1)
                    for t in range(GT):
                        ins = v.tensor_scalar(qn[:, g % 2, t, :], psum[:, 2 + t // 2, D * (t % 2):D * (t % 2) + D],
                                              qmv[:, t, 0:1], qrs[:, t:t + 1], ALU.subtract, ALU.mult)
                    ins.then_inc(sem("x0_qn"), 1)

                def output_rows(g):
                    ve.wait_ge(sem("x0_out"), g + 1)
                    for j in range(2):
                        ins = v.tensor_tensor(yb[:, 2 * j:2 * j + 2, :], psum[:, 6 + j, :].rearrange("p (t n) -> p t n", t=2),
                                              bc(bd[:, :], 2), ALU.add)
                    ins.then_inc(sem("x0_y"), 1)
                    ve.wait_ge(sem("x0_y"), g + 1)
                    row_stats(lambda t: yb[:, t, :], GT, "x0_var1")
                    ve.wait_ge(sem("x0_rstd1"), g + 1)
                    for t in range(GT):
                        ins = v.tensor_scalar(yb[:, t, :], yb[:, t, :], qmv[:, GT + t, 0:1], qrs[:, GT + t:GT + t + 1],
                                              ALU.subtract, ALU.mult)
                    V(ins)
                    V.sync()
                    V(v.tensor_tensor(yb, yb, bc(gB[:, :], GT), ALU.mult))
                    V.sync()
                    ve.wait_ge(sem("beta_added"), g + 1)
                    V(v.tensor_tensor(x[:, GT * g:GT * g + GT, :], yb, x[:, GT * g:GT * g + GT, :], ALU.add))
                    group_stats(g, nxt)

                normalise(1, "x0")
                query_stats(0)
                query_norm(0)
                for g in range(G):
                    ve.wait_ge(sem("x0_affine"), g + 1)
                    cols = qT[:, :, GN * (g % 2):GN * (g % 2) + GN]
                    v.tensor_scalar(cols, cols, 0.0, X_EPS, ALU.max, ALU.add).then_inc(sem("x0_qT"), 1)
                    if g + 1 < G:
                        query_stats(g + 1)
                        if g + 2 < G:
                            normalise(g + 2, "x0")
                        query_norm(g + 1)
                    if g == 2:
                        output_rows(1)
                    if g == 3:
                        for gg in range(2):
                            ffn_rows(gg)
                    if g % 2 == 0:
                        continue
                    for half in range(2):
                        ve.wait_ge(sem("x0_kv"), 2 * (g // 2) + half + 1)
                        for i in range(0, NK, 3):
                            n = min(3, NK - i)
                            bank, _ = kv_place(half, i)
                            rows = psum[:, bank, 0:2 * KV * n].rearrange("p (i k c) -> p i k c", k=K, c=KV)
                            ins = v.tensor_scalar(zden[:, half, NK * i:NK * (i + n)].rearrange("p (i k t) -> p i k t", k=K, t=4),
                                                  rows[:, :, :, 4 * HD:KV], X_EPS, None, ALU.add)
                        V(ins)
                        V.sync()
                        V(v.reciprocal(zden[:, half], zden[:, half]))
                        V.sync()
                        for i in range(NK):
                            bank, lo = kv_place(half, i)
                            col = HD * (NK * half + i)
                            rows = psum[:, bank, lo:lo + 2 * KV].rearrange("p (k c) -> p k c", k=K)[:, :, 0:4 * HD]
                            ins = v.tensor_tensor(att[:, :, col:col + HD].rearrange("p (k t) e -> p k t e", k=K),
                                                  rows.rearrange("p k (t e) -> p k t e", e=HD),
                                                  bc(zden[:, half, NK * i:NK * i + NK], HD, 2).rearrange("p (k t) e -> p k t e", k=K), ALU.mult)
                        ins.then_inc(sem("x0_att"), 1)
                    for gg in (0,) if g == 1 else (2, 3):
                        output_rows(gg)

            def global_scale(n, maxima, cols, c):
                V.sync()
                v.tensor_reduce(sc[:, 0:1], maxima, AX, ALU.max).then_inc(sem("gm_col"), 1)
                ve.wait_ge(sem("gm_row"), n + 1)
                v.tensor_reduce(sc[0:1, 1:2], psum[0:1, 7, 0:P], AX, ALU.max).then_inc(sem("gm_one"), 1)
                ve.wait_ge(sem("gm_all"), n + 1)
                s_col, inv = sc[:, cols:cols + 1], sc[:, cols + 1:cols + 2]
                V(v.tensor_scalar(s_col, psum[:, 7, 256:257], c, 1.0 / QMAX, ALU.mult, ALU.mult))
                V.sync()
                V(v.tensor_scalar(s_col, s_col, TINY, None, ALU.max))
                V.sync()
                V(v.reciprocal(inv, s_col))
                V.sync()
                V(v.tensor_scalar(inv, inv, c, None, ALU.mult))
                V.sync()

            MAGIC = 12582912.0

            def ffn(nxt):
                SX, SU, SG, SP, SO, CP, CR = 10, 15, 20, 25, 30, 35, 36
                for g in (2, 3):
                    ffn_rows(g)
                global_scale(0, am[:, 0:G], SX, 1.0)
                for g in range(G):
                    rows = at(1024 * g, 1024)
                    V(v.tensor_scalar(rows, rows, sc[:, SX + 1:SX + 2], MAGIC, ALU.mult, ALU.add))
                    V.sync()
                    v.tensor_scalar(rows, rows, -MAGIC, None, ALU.add).then_inc(sem("xq_ready"), 1)

                def product_max(m, a, b):
                    V(v.tensor_tensor(act[:, m, :], a, b, ALU.mult))
                    V.sync()
                    V(v.tensor_reduce(am[:, m:m + 1], act[:, m, :], AX, ALU.max, apply_absolute_value=True))

                def split_low(step):
                    g = step % G
                    ve.wait_ge(sem("f_high"), step + 1)
                    v.tensor_tensor(xhl[:, step % 2, 1, :, :], xqT[:, :, GN * g:GN * g + GN], xhl[:, step % 2, 0, :, :].bitcast(F32),
                                    ALU.subtract).then_inc(sem("f_low"), 1)

                def unit_maxima(first, ahead):
                    for n in range(first, first + FM * G):
                        step, m = divmod(n, FM)
                        if m == 0 and ahead <= step + 1 < 2 * G:
                            split_low(step + 1)
                        ve.wait_ge(sem("f_evac"), n + 1)
                        ins = v.tensor_reduce(am[:, n:n + 1], act[:, m, GN * (step % G):GN * (step % G) + GN], AX, ALU.max, apply_absolute_value=True)
                    V(ins)

                split_low(0)
                unit_maxima(0, 1)
                split_low(G + 1)
                global_scale(1, am[:, 0:FM * G], SU, sc[:, SX:SX + 1])
                for g in range(G):
                    cols = slice(GN * g, GN * g + GN)
                    v.tensor_scalar(qup[:, :, cols], act[:, :, cols], sc[:, SU + 1:SU + 2], None, ALU.mult).then_inc(sem("qup_ready"), 1)
                unit_maxima(FM * G, G + 2)
                global_scale(2, am[:, FM * G:2 * FM * G], SG, sc[:, SX:SX + 1])
                v.tensor_scalar(qgate[:, 0, :], act[:, 0, :], sc[:, SG + 1:SG + 2], None, ALU.mult).then_inc(sem("qgate_ready"), 1)
                V(v.tensor_scalar(sc[:, CP:CP + 1], sc[:, SG:SG + 1], 1.0 / 65536.0, None, ALU.mult))
                for m in range(FM):
                    ve.wait_ge(sem("sigmoid_ready"), m + 1)
                    V(v.tensor_scalar(zint[:, m % 4, :], act[:, m, :], 65536.0, 65535.0, ALU.mult, ALU.min))
                    V.sync()
                    product_max(m, zint[:, m % 4, :], qgate[:, m, :])
                global_scale(3, am[:, 0:FM], SP, sc[:, CP:CP + 1])
                v.tensor_scalar(sc[:, CR:CR + 1], sc[:, SP:SP + 1], sc[:, SU:SU + 1], None, ALU.mult).then_inc(sem("p_scaled"), 1)
                for m in range(FM):
                    ve.wait_ge(sem("qp_ready"), m + 1)
                    product_max(m, qgate[:, m, :], qup[:, m, :])
                global_scale(4, am[:, 0:FM], SO, sc[:, CR:CR + 1])
                for g in range(G):
                    cols = act[:, :, GN * g:GN * g + GN]
                    V(v.tensor_scalar(cols, cols, sc[:, SO + 1:SO + 2], MAGIC, ALU.mult, ALU.add))
                    V.sync()
                    v.tensor_scalar(cols, cols, -MAGIC, None, ALU.add).then_inc(sem("q3_ready"), 1)
                for u in range(2 * G):
                    ve.wait_ge(sem("down_mm"), u + 1)
                    v.scalar_tensor_tensor(out=x[:, 2 * u:2 * u + 2, :], in0=psum[:, u % 4, :].rearrange("p (t n) -> p t n", t=2),
                                           scalar=sc[:, SO:SO + 1], in1=x[:, 2 * u:2 * u + 2, :],
                                           op0=ALU.mult, op1=ALU.add).then_inc(sem("down_drained"), 1)
                    if u % 2:
                        ve.wait_ge(sem("down_drained"), u + 1)
                        group_stats(u // 2, nxt)
                    if u == 5:
                        normalise(0, nxt)

            def cross1(nxt):
                normalise(1, "x1")
                for g in range(G):
                    ve.wait_ge(sem("x1_scores"), g + 1)
                    V(v.tensor_reduce(qve[:, GT:2 * GT], psum[:, 2, 0:GT * C].rearrange("p (t c) -> p t c", t=GT), AX, ALU.max, negate=True))
                    V.sync()
                    v.tensor_scalar(qve[:, 0:GT], qve[:, GT:2 * GT], D ** -0.5, None, ALU.mult).then_inc(sem("x1_max"), 1)
                    if g + 2 < G:
                        normalise(g + 2, "x1")
                    ve.wait_ge(sem("x1_exp"), g + 1)
                    V(v.reciprocal(qrs[:, GT:2 * GT], qrs[:, 0:GT]))
                    V.sync()
                    ve.wait_ge(sem("x1_out"), g + 1)
                    for t in range(GT):
                        tt = GT * g + t
                        ins = v.scalar_tensor_tensor(out=x[:, tt, :], in0=psum[:, 6 + t // 2, D * (t % 2):D * (t % 2) + D],
                                                     scalar=qrs[:, GT + t:GT + t + 1], in1=x[:, tt, :], op0=ALU.mult, op1=ALU.add)
                    ins.then_inc(sem("x1_added"), 1)
                    ve.wait_ge(sem("x1_added"), g + 1)
                    group_stats(g, nxt)
                    if g == G - 2:
                        normalise(0, nxt)

            def experts():
                def low_parts(g):
                    ve.wait_ge(sem("xT_ready"), G * TURN["m1"] + g + 1)
                    if g >= 2:
                        ve.wait_ge(sem("m1_mm"), 16 * (g - 1))
                    for k in range(K):
                        ins = v.tensor_tensor(xhl[:, g % 2, 1, k, :], psum[:, k, :], xhl[:, g % 2, 0, k, :].bitcast(F32), ALU.subtract)
                    ins.then_inc(sem("m1_low"), 1)

                def routing(g):
                    ve.wait_ge(sem("m1_logits"), g + 1)
                    V(v.tensor_tensor(lg, psum[:, 2, 0:GT * E].rearrange("p (t e) -> p t e", t=GT), bc(rb[:, :], GT), ALU.add))
                    V.sync()
                    V(v.tensor_reduce(lm, lg, AX, ALU.max))
                    V.sync()
                    V(v.tensor_tensor(ex, lg, bc(lm, E, 2), ALU.subtract))
                    V.sync()
                    V(v.tensor_scalar(best[:, g % 2], ex, 0.0, None, ALU.is_equal))
                    V.sync()
                    v.tensor_tensor(mw, best[:, g % 2], bc(rank[:, :], GT), ALU.mult).then_inc(sem("m1_shift"), 1)
                    ve.wait_ge(sem("m1_shift"), g + 1)
                    V(v.tensor_reduce(lm, mw, AX, ALU.max))
                    V.sync()
                    V(v.tensor_tensor(best[:, g % 2], mw, bc(lm, E, 2), ALU.is_equal))
                    ve.wait_ge(sem("m1_exp"), g + 1)
                    V.sync()
                    V(v.tensor_reduce(lm, ex, AX, ALU.add))
                    V.sync()
                    V(v.reciprocal(lm, lm))
                    V.sync()
                    v.tensor_tensor(mw, best[:, g % 2], bc(lm, E, 2), ALU.mult).then_inc(sem("m1_mw"), 1)
                    ve.wait_ge(sem("m1_mw"), g + 1)
                    V(v.tensor_copy(best[:, g % 2], mw))
                    V.sync()

                def add_bias(g):
                    ve.wait_ge(sem("m1_bias"), g + 1)
                    for j in range(2):
                        t0 = GT * g + 2 * j
                        ins = v.tensor_tensor(x[:, t0:t0 + 2, :], psum[:, 2 + j, :].rearrange("p (t n) -> p t n", t=2),
                                              x[:, t0:t0 + 2, :], ALU.add)
                    V(ins)
                    V.sync()
                    ve.sem_inc(sem("m1_bias_added"), 1)

                def add_experts(g, t):
                    for c in range(E // 2):
                        n = 16 * g + 4 * t + c
                        ve.wait_ge(sem("m1_mm"), n + 1)
                        for e in (2 * c, 2 * c + 1):
                            ins = v.scalar_tensor_tensor(out=x[:, GT * g + t, :], in0=psum[:, 4 + n % 4, D * (e % 2):D * (e % 2) + D],
                                                         scalar=best[:, g % 2, t, e:e + 1], in1=x[:, GT * g + t, :], op0=ALU.mult, op1=ALU.add)
                            if e % 2 == 0:
                                V(ins)
                                V.sync()
                        ins.then_inc(sem("m1_added"), 1)
                        ve.wait_ge(sem("m1_added"), n + 1)

                low_parts(0)
                normalise(1, "m1")
                routing(0)
                low_parts(1)
                add_bias(0)
                for g in range(G):
                    add_experts(g, 0)
                    if g + 1 < G:
                        routing(g + 1)
                    add_experts(g, 1)
                    if g + 2 < G:
                        normalise(g + 2, "m1")
                    add_experts(g, 2)
                    add_experts(g, 3)
                    if g + 1 < G:
                        add_bias(g + 1)
                    if g + 2 < G:
                        low_parts(g + 2)
                    ve.sem_inc(sem("moe_done"), 1)

            qkv(0)
            attention(0)
            weights_low()
            context_products()
            project(0, "x0")
            cross0("f0")
            ffn("q1")
            qkv(1)
            attention(1)
            project(1, "x1")
            cross1("m1")
            experts()


def rope_tables():
    inv = (1.0 / 10000.0 ** (np.arange(0, HD, 2, dtype=np.float32) / HD)).astype(np.float32)
    f = np.arange(H, dtype=np.float32)[:, None] * inv[None, :]
    cos, sin = np.cos(f), np.sin(f)
    c = np.concatenate([cos, cos], axis=1).reshape(-1)
    s = np.concatenate([-sin, sin], axis=1).reshape(-1)
    return np.tile(c, 2), np.tile(s, 2)


def kernel(x, ctx_1024, mask_BxS2_ff1, L0_attn_qkv_w, L0_attn_qkv_b, L0_attn_out_w, L0_attn_out_b,
           L0_xattn_wq, L0_xattn_wk, L0_xattn_wv, L0_xattn_ln_gamma, L0_xattn_ln_beta, L0_xattn_dense_w,
           L0_xattn_dense_b, L0_ffn_w_gate, L0_ffn_w_up, L0_ffn_w_down, L1_attn_W_attn, L1_attn_b_attn,
           L1_attn_W_proj, L1_attn_b_proj, L1_xattn_Wq, L1_xattn_Wkv, L1_ffn_router_w, L1_ffn_router_b,
           L1_ffn_expert_w, L1_ffn_expert_b):
    import concourse.bacc as bacc
    from concourse.bass_utils import run_bass_kernel_spmd

    def halves(w):
        w = np.asarray(w)
        return w.reshape(-1, P, w.shape[-1]).transpose(1, 0, 2)

    def columns(v):
        return np.asarray(v).reshape(-1, P).T

    def split_qkv(w):
        w = np.asarray(w)
        w = w.reshape(w.shape[:-1] + (H, 3, HD))
        return w[..., 0, :].reshape(w.shape[:-3] + (D,)), w[..., 1, :].reshape(w.shape[:-3] + (D,)), w[..., 2, :].reshape(w.shape[:-3] + (D,))

    def swap(w):
        r = w.reshape(w.shape[:-1] + (-1, 2, HD // 2))
        return r[..., ::-1, :].reshape(w.shape)

    arrays = {}
    arrays["x"] = np.asarray(x).reshape(T, P, D).transpose(1, 0, 2)
    for i, (w, bias, wo, bo) in enumerate(((L0_attn_qkv_w, L0_attn_qkv_b, L0_attn_out_w, L0_attn_out_b),
                                           (L1_attn_W_attn, L1_attn_b_attn, L1_attn_W_proj, L1_attn_b_proj))):
        q, k, vv = split_qkv(w)
        qk = np.concatenate([q, k], axis=1)
        qb, kb, vb = split_qkv(bias)
        bqk = np.concatenate([qb, kb])
        arrays[f"wqk{i}"], arrays[f"wv{i}"], arrays[f"bqk{i}"], arrays[f"bv{i}"] = halves(qk), halves(vv), columns(bqk), vb
        arrays[f"wo{i}"], arrays[f"bo{i}"] = halves(wo), np.asarray(bo)
        if i == 0:
            arrays["wqks"], arrays["bqks"] = halves(swap(qk)), columns(swap(bqk))
    cos, sin = rope_tables()
    arrays["cos"], arrays["sin"] = np.tile(cos, (P, 1)), np.tile(sin, (P, 1))
    arrays["coscol"], arrays["sincol"] = columns(cos), columns(sin)
    arrays["ctxT"] = halves(np.asarray(ctx_1024).reshape(B * C, D).T)
    arrays["mask"] = np.asarray(mask_BxS2_ff1).T
    arrays["xwq"] = halves(L0_xattn_wq)
    arrays["xwkv"] = halves(np.concatenate([np.asarray(L0_xattn_wk), np.asarray(L0_xattn_wv)], axis=1))
    arrays["xwd"] = halves(L0_xattn_dense_w)
    arrays["g"], arrays["b"], arrays["bd"] = (np.asarray(a) for a in (L0_xattn_ln_gamma, L0_xattn_ln_beta, L0_xattn_dense_b))
    arrays["gcol"], arrays["bcol"] = columns(L0_xattn_ln_gamma), columns(L0_xattn_ln_beta)
    head = np.arange(D) // HD
    same = np.concatenate([head[:, None] == head[None, :], head[:, None] == np.arange(H)[None, :]], axis=1)
    pick = np.zeros((B * H, B, D), np.float32)
    for b in range(B):
        pick[b * H + head, b, np.arange(D)] = 1.0
    arrays["pick"] = np.concatenate([pick, pick], axis=0)
    arrays["dmask"] = halves(same.astype(np.float32))
    arrays["w1q"] = halves(np.asarray(L1_xattn_Wq).T)
    arrays["w1kv"] = halves(L1_xattn_Wkv)
    flat = lambda w: halves(w).reshape(P, -1)
    arrays["ffw"] = np.concatenate([flat(L0_ffn_w_gate), flat(L0_ffn_w_up), flat(L0_ffn_w_down)], axis=1)
    arrays["rw"] = halves(np.asarray(L1_ffn_router_w).T)
    arrays["rb"], arrays["eb"] = np.asarray(L1_ffn_router_b), np.asarray(L1_ffn_expert_b)
    arrays["we"] = halves(np.asarray(L1_ffn_expert_w).transpose(2, 0, 1).reshape(D, E * D))
    arrays["rank"] = np.tile(np.arange(E, 0, -1, dtype=np.float32), (P, 1))
    arrays["ident"] = np.eye(P, dtype=np.float32)
    arrays["identb"] = np.eye(P, dtype=mybir.dt.np(BF16))
    above = np.triu(np.full((P, P), NEG, np.float32), 1)
    arrays["causal"] = np.stack([above, above.T], axis=1).astype(mybir.dt.np(BF16))

    nc = bacc.Bacc("TRN2", target_bir_lowering=False, num_devices=1)
    dram, given = {}, {}
    for name, a in arrays.items():
        given[f"in_{name}"] = np.ascontiguousarray(a)
        dram[name] = nc.dram_tensor(f"in_{name}", a.shape, mybir.dt.from_np(a.dtype), kind="ExternalInput").ap()
    out = nc.dram_tensor("out", (P, T, D), F32, kind="ExternalOutput").ap()
    build(nc, dram, out)
    r = run_bass_kernel_spmd(nc, [given], core_ids=[0])
    return np.asarray(r.results[0]["out"]).transpose(1, 0, 2).reshape(B, S, D)
```
